# Optimizing a Trainium2 kernel written in Bass

```python
import numpy as np
import jax
import jax.numpy as jnp

def _softmax(x, axis=-1):
    return jax.nn.softmax(x, axis=axis)

def _gelu(x):
    return jax.nn.gelu(x, approximate=True)

def _silu(x):
    return jax.nn.silu(x)

def _sigmoid(x):
    return jax.nn.sigmoid(x)

def _layernorm(x, axis=-1, eps=1e-05):
    m = jnp.mean(x, axis=axis, keepdims=True)
    v = jnp.var(x, axis=axis, keepdims=True)
    return (x - m) / jnp.sqrt(v + eps)

def _scatter_add(tgt, idx, src, axis=0):
    return tgt.at[idx].add(src)

def _segment_sum(src, seg, n):
    return jax.ops.segment_sum(src, seg, n)
kernel_name = 'mk_dlrm_tower_d1_rec_r8_ac7088'

def setup_inputs(seed: int=0):
    np.random.seed(seed)
    _w = jnp.asarray

    def _rec_inputs():
        import jax
        import jax.numpy as jnp
        _tk = jax.random.key(seed)
        dense_ctx = jax.random.normal(jax.random.fold_in(_tk, 190), (512, 16), jnp.float32)
        ids = jnp.stack([jax.random.randint(jax.random.fold_in(_tk, 200 + f), (512,), 0, v, jnp.int32) for f, v in enumerate([1250, 12500, 125000, 12500, 125000, 12500, 12500, 1000, 1000, 12500, 1000, 125000, 125000, 12500, 125000, 125000, 1000, 1000, 12500, 1000, 125000, 1250, 1000, 1000, 1250, 1250, 1250, 1250, 1000, 1250, 1250, 1000])], axis=1)
        tbl_0 = 0.05 * jax.random.normal(jax.random.fold_in(_tk, 500 + 0), (1250, 32), jnp.float32)
        tbl_1 = 0.05 * jax.random.normal(jax.random.fold_in(_tk, 500 + 1), (12500, 32), jnp.float32)
        tbl_2 = 0.05 * jax.random.normal(jax.random.fold_in(_tk, 500 + 2), (125000, 32), jnp.float32)
        tbl_3 = 0.05 * jax.random.normal(jax.random.fold_in(_tk, 500 + 3), (12500, 32), jnp.float32)
        tbl_4 = 0.05 * jax.random.normal(jax.random.fold_in(_tk, 500 + 4), (125000, 32), jnp.float32)
        tbl_5 = 0.05 * jax.random.normal(jax.random.fold_in(_tk, 500 + 5), (12500, 32), jnp.float32)
        tbl_6 = 0.05 * jax.random.normal(jax.random.fold_in(_tk, 500 + 6), (12500, 32), jnp.float32)
        tbl_7 = 0.05 * jax.random.normal(jax.random.fold_in(_tk, 500 + 7), (1000, 32), jnp.float32)
        tbl_8 = 0.05 * jax.random.normal(jax.random.fold_in(_tk, 500 + 8), (1000, 32), jnp.float32)
        tbl_9 = 0.05 * jax.random.normal(jax.random.fold_in(_tk, 500 + 9), (12500, 32), jnp.float32)
        tbl_10 = 0.05 * jax.random.normal(jax.random.fold_in(_tk, 500 + 10), (1000, 32), jnp.float32)
        tbl_11 = 0.05 * jax.random.normal(jax.random.fold_in(_tk, 500 + 11), (125000, 32), jnp.float32)
        tbl_12 = 0.05 * jax.random.normal(jax.random.fold_in(_tk, 500 + 12), (125000, 32), jnp.float32)
        tbl_13 = 0.05 * jax.random.normal(jax.random.fold_in(_tk, 500 + 13), (12500, 32), jnp.float32)
        tbl_14 = 0.05 * jax.random.normal(jax.random.fold_in(_tk, 500 + 14), (125000, 32), jnp.float32)
        tbl_15 = 0.05 * jax.random.normal(jax.random.fold_in(_tk, 500 + 15), (125000, 32), jnp.float32)
        tbl_16 = 0.05 * jax.random.normal(jax.random.fold_in(_tk, 500 + 16), (1000, 32), jnp.float32)
        tbl_17 = 0.05 * jax.random.normal(jax.random.fold_in(_tk, 500 + 17), (1000, 32), jnp.float32)
        tbl_18 = 0.05 * jax.random.normal(jax.random.fold_in(_tk, 500 + 18), (12500, 32), jnp.float32)
        tbl_19 = 0.05 * jax.random.normal(jax.random.fold_in(_tk, 500 + 19), (1000, 32), jnp.float32)
        tbl_20 = 0.05 * jax.random.normal(jax.random.fold_in(_tk, 500 + 20), (125000, 32), jnp.float32)
        tbl_21 = 0.05 * jax.random.normal(jax.random.fold_in(_tk, 500 + 21), (1250, 32), jnp.float32)
        tbl_22 = 0.05 * jax.random.normal(jax.random.fold_in(_tk, 500 + 22), (1000, 32), jnp.float32)
        tbl_23 = 0.05 * jax.random.normal(jax.random.fold_in(_tk, 500 + 23), (1000, 32), jnp.float32)
        tbl_24 = 0.05 * jax.random.normal(jax.random.fold_in(_tk, 500 + 24), (1250, 32), jnp.float32)
        tbl_25 = 0.05 * jax.random.normal(jax.random.fold_in(_tk, 500 + 25), (1250, 32), jnp.float32)
        tbl_26 = 0.05 * jax.random.normal(jax.random.fold_in(_tk, 500 + 26), (1250, 32), jnp.float32)
        tbl_27 = 0.05 * jax.random.normal(jax.random.fold_in(_tk, 500 + 27), (1250, 32), jnp.float32)
        tbl_28 = 0.05 * jax.random.normal(jax.random.fold_in(_tk, 500 + 28), (1000, 32), jnp.float32)
        tbl_29 = 0.05 * jax.random.normal(jax.random.fold_in(_tk, 500 + 29), (1250, 32), jnp.float32)
        tbl_30 = 0.05 * jax.random.normal(jax.random.fold_in(_tk, 500 + 30), (1250, 32), jnp.float32)
        tbl_31 = 0.05 * jax.random.normal(jax.random.fold_in(_tk, 500 + 31), (1000, 32), jnp.float32)
        _rk = jax.random.fold_in(_tk, 7)
        W_top1 = 0.0606339 * jax.random.normal(jax.random.fold_in(_tk, 801), (272, 512), jnp.float32)
        W_top2 = 0.0441942 * jax.random.normal(jax.random.fold_in(_tk, 802), (512, 256), jnp.float32)
        W_top3 = 0.0625 * jax.random.normal(jax.random.fold_in(_tk, 803), (256, 1), jnp.float32)
        b_top1 = jnp.zeros((512,), jnp.float32)
        b_top2 = jnp.zeros((256,), jnp.float32)
        return (dense_ctx, ids, tbl_0, tbl_1, tbl_2, tbl_3, tbl_4, tbl_5, tbl_6, tbl_7, tbl_8, tbl_9, tbl_10, tbl_11, tbl_12, tbl_13, tbl_14, tbl_15, tbl_16, tbl_17, tbl_18, tbl_19, tbl_20, tbl_21, tbl_22, tbl_23, tbl_24, tbl_25, tbl_26, tbl_27, tbl_28, tbl_29, tbl_30, tbl_31, W_top1, b_top1, W_top2, b_top2, W_top3)
    dense_ctx, ids, tbl_0, tbl_1, tbl_2, tbl_3, tbl_4, tbl_5, tbl_6, tbl_7, tbl_8, tbl_9, tbl_10, tbl_11, tbl_12, tbl_13, tbl_14, tbl_15, tbl_16, tbl_17, tbl_18, tbl_19, tbl_20, tbl_21, tbl_22, tbl_23, tbl_24, tbl_25, tbl_26, tbl_27, tbl_28, tbl_29, tbl_30, tbl_31, W_top1, b_top1, W_top2, b_top2, W_top3 = _rec_inputs()

    def _L0_rec_setup():
        import jax, jax.numpy as jnp
        import numpy as np
        B, F, D = (512, 32, 32)
        LAYER_SIZE = [128, 128]

        def _cin_forward(inputs, filters):
            x0 = inputs
            prev = inputs
            outs = []
            for W in filters:
                z = jnp.einsum('bhd,bmd->bhmd', x0, prev)
                b, h, m, d = z.shape
                z = z.reshape(b, h * m, d)
                cur = jnp.einsum('bpd,pn->bnd', z, W[0])
                cur = jax.nn.relu(cur)
                prev = cur
                outs.append(cur)
            result = jnp.concatenate(outs, axis=1)
            return jnp.sum(result, axis=-1)
        key = jax.random.key(seed)
        k1, k2, k3 = jax.random.split(key, 3)
        inputs = jax.random.normal(k1, (B, F, D), dtype=jnp.float32)
        field_nums = [F] + LAYER_SIZE
        filter_0 = jax.random.normal(k2, (1, field_nums[0] * field_nums[0], field_nums[1]), dtype=jnp.float32) * 0.05
        filter_1 = jax.random.normal(k3, (1, field_nums[0] * field_nums[1], field_nums[2]), dtype=jnp.float32) * 0.05
        return {'inputs': inputs, 'filter_0': filter_0, 'filter_1': filter_1}
    _L0_rec_all = _L0_rec_setup()
    _L0_rec_in = {k: v for k, v in _L0_rec_all.items() if k in ('filter_0', 'filter_1')}
    del _L0_rec_all
    return {'dense_ctx': dense_ctx, 'ids': ids, 'tbl_0': tbl_0, 'tbl_1': tbl_1, 'tbl_2': tbl_2, 'tbl_3': tbl_3, 'tbl_4': tbl_4, 'tbl_5': tbl_5, 'tbl_6': tbl_6, 'tbl_7': tbl_7, 'tbl_8': tbl_8, 'tbl_9': tbl_9, 'tbl_10': tbl_10, 'tbl_11': tbl_11, 'tbl_12': tbl_12, 'tbl_13': tbl_13, 'tbl_14': tbl_14, 'tbl_15': tbl_15, 'tbl_16': tbl_16, 'tbl_17': tbl_17, 'tbl_18': tbl_18, 'tbl_19': tbl_19, 'tbl_20': tbl_20, 'tbl_21': tbl_21, 'tbl_22': tbl_22, 'tbl_23': tbl_23, 'tbl_24': tbl_24, 'tbl_25': tbl_25, 'tbl_26': tbl_26, 'tbl_27': tbl_27, 'tbl_28': tbl_28, 'tbl_29': tbl_29, 'tbl_30': tbl_30, 'tbl_31': tbl_31, 'W_top1': W_top1, 'b_top1': b_top1, 'W_top2': W_top2, 'b_top2': b_top2, 'W_top3': W_top3, 'L0_rec_filter_0': _L0_rec_in['filter_0'], 'L0_rec_filter_1': _L0_rec_in['filter_1']}

def reference(dense_ctx, ids, tbl_0, tbl_1, tbl_2, tbl_3, tbl_4, tbl_5, tbl_6, tbl_7, tbl_8, tbl_9, tbl_10, tbl_11, tbl_12, tbl_13, tbl_14, tbl_15, tbl_16, tbl_17, tbl_18, tbl_19, tbl_20, tbl_21, tbl_22, tbl_23, tbl_24, tbl_25, tbl_26, tbl_27, tbl_28, tbl_29, tbl_30, tbl_31, W_top1, b_top1, W_top2, b_top2, W_top3, L0_rec_filter_0, L0_rec_filter_1):
    import jax
    import jax.numpy as jnp

    def _L0_rec_ref(inputs, filter_0, filter_1):
        import jax, jax.numpy as jnp
        import numpy as np
        B, F, D = (512, 32, 32)
        LAYER_SIZE = [128, 128]

        def _cin_forward(inputs, filters):
            x0 = inputs
            prev = inputs
            outs = []
            for W in filters:
                z = jnp.einsum('bhd,bmd->bhmd', x0, prev)
                b, h, m, d = z.shape
                z = z.reshape(b, h * m, d)
                cur = jnp.einsum('bpd,pn->bnd', z, W[0])
                cur = jax.nn.relu(cur)
                prev = cur
                outs.append(cur)
            result = jnp.concatenate(outs, axis=1)
            return jnp.sum(result, axis=-1)
        return _cin_forward(inputs, (filter_0, filter_1))
    e = jnp.stack([tbl_0[ids[:, 0]], tbl_1[ids[:, 1]], tbl_2[ids[:, 2]], tbl_3[ids[:, 3]], tbl_4[ids[:, 4]], tbl_5[ids[:, 5]], tbl_6[ids[:, 6]], tbl_7[ids[:, 7]], tbl_8[ids[:, 8]], tbl_9[ids[:, 9]], tbl_10[ids[:, 10]], tbl_11[ids[:, 11]], tbl_12[ids[:, 12]], tbl_13[ids[:, 13]], tbl_14[ids[:, 14]], tbl_15[ids[:, 15]], tbl_16[ids[:, 16]], tbl_17[ids[:, 17]], tbl_18[ids[:, 18]], tbl_19[ids[:, 19]], tbl_20[ids[:, 20]], tbl_21[ids[:, 21]], tbl_22[ids[:, 22]], tbl_23[ids[:, 23]], tbl_24[ids[:, 24]], tbl_25[ids[:, 25]], tbl_26[ids[:, 26]], tbl_27[ids[:, 27]], tbl_28[ids[:, 28]], tbl_29[ids[:, 29]], tbl_30[ids[:, 30]], tbl_31[ids[:, 31]]], axis=1)
    z = _L0_rec_ref(e, L0_rec_filter_0, L0_rec_filter_1)
    z = z.reshape(z.shape[0], -1)
    h = jnp.concatenate([z, dense_ctx], axis=1)
    h = jnp.maximum(h @ W_top1 + b_top1, 0.0)
    h = jnp.maximum(h @ W_top2 + b_top2, 0.0)
    y = h @ W_top3
    return y

_drawn_inputs = setup_inputs


def setup_inputs(seed=0):
    import zlib

    import numpy as np

    out = dict(_drawn_inputs(seed))
    spreads = {'b_top1': (0.0, 0.427), 'b_top2': (0.0, 0.416)}
    factors = {'tbl_0': 6.016,
     'tbl_1': 6.126,
     'tbl_2': 6.257,
     'tbl_3': 6.093,
     'tbl_4': 6.397,
     'tbl_5': 5.732,
     'tbl_6': 6.371,
     'tbl_7': 5.991,
     'tbl_8': 6.039,
     'tbl_9': 6.217,
     'tbl_10': 5.773,
     'tbl_11': 6.293,
     'tbl_12': 6.117,
     'tbl_13': 5.722,
     'tbl_14': 5.964,
     'tbl_15': 6.024,
     'tbl_16': 6.165,
     'tbl_17': 5.616,
     'tbl_18': 5.933,
     'tbl_19': 6.176,
     'tbl_20': 6.226,
     'tbl_21': 5.752,
     'tbl_22': 6.295,
     'tbl_23': 6.071,
     'tbl_24': 6.362,
     'tbl_25': 5.978,
     'tbl_26': 5.953,
     'tbl_27': 5.986,
     'tbl_28': 6.181,
     'tbl_29': 6.289,
     'tbl_30': 6.228,
     'tbl_31': 5.837,
     'L0_rec_filter_1': 8.0}
    for name, (base, spread) in spreads.items():
        noise = np.random.default_rng([zlib.crc32(name.encode()), seed]).standard_normal(out[name].shape)
        drawn = base * np.exp(spread * noise) if base else spread * noise
        out[name] = jnp.asarray(drawn.astype(out[name].dtype))
    for name, factor in factors.items():
        out[name] = (out[name] * factor).astype(out[name].dtype)
    return out
```

```python
from contextlib import ExitStack

import numpy as np

import concourse.bass as bass
from concourse import mybir

BATCH, FIELDS, DIM, MAPS = 512, 32, 32, 128
DENSE, HID1, HID2 = 16, 512, 256
P = 128
TILES = BATCH // P
D_GROUP = 4
GROUPS_TILE = DIM // D_GROUP
GROUPS = TILES * GROUPS_TILE
CHUNKS = GROUPS * D_GROUP
SHIFTS = FIELDS // 2
TAIL = FIELDS // 2
KQ = SHIFTS * FIELDS // P
BANK = 512
H_BANK = BANK // MAPS
HQ = FIELDS // H_BANK
LOW_ROW = 3 * FIELDS
TAIL_ROW = 2 * FIELDS

ACT_BANKS = (0, 2, 4, 6)
DVE_BANKS = tuple(hq for hq in range(HQ) if hq not in ACT_BANKS)
ACT_C, DVE_C = len(ACT_BANKS), len(DVE_BANKS)
ACT_N, DVE_N = D_GROUP * ACT_C, D_GROUP * DVE_C
ACT_RING, DVE_RING, PROD_RING = 2, 4, 2 * ACT_C
STT_N = DVE_N * H_BANK
SUM_N = 2 * D_GROUP
assert ACT_C == 4 and ACT_N % ACT_RING == 0 and DVE_N % DVE_RING == 0 and ACT_N % PROD_RING == 0

TURN_AT = {(0, 0): 0, (0, 3): 1, (0, 6): 2, (1, 3): 3, (1, 7): 4, (2, 3): 5}
USES = 2 + KQ
L1_AT = {(1, 1): 0, (1, 5): 1, (2, 1): 2, (2, 5): 3, (2, 7): 4}
HIGH_AT, LOW_AT = (3, 0), (3, 1)
BLOCKS = 4
F_BLOCK = FIELDS // BLOCKS
EARLY = slice(0, TILES - 1)
LATE = slice(TILES - 1, TILES)


def mlp_part(tiles):
    return 0 if tiles == EARLY else 1


def cin_tower(nc, dense, ids, tables, w_top1, b_top1, w_top2, b_top2, w_top3, w0_a, w0_b, select, w1, out):
    f32, f32r, i32 = mybir.dt.float32, mybir.dt.float32r, mybir.dt.int32
    ALU, ACT = mybir.AluOpType, mybir.ActivationFunctionType

    with ExitStack() as ctx:
        def sb(name, shape, dt=f32):
            return ctx.enter_context(nc.sbuf_tensor("sb_" + name, shape, dt))

        def sem(name):
            return ctx.enter_context(nc.semaphore(name))

        ids_sb = sb("ids", [P, TILES, FIELDS], i32)
        ids_next = sb("ids_next", [P, FIELDS], i32)
        rows_next = sb("rows_next", [P, FIELDS, DIM])
        emb = sb("emb", [P, DIM, FIELDS])
        xs = sb("xs", [P, 2, D_GROUP, FIELDS])
        tail_raw = sb("tail_raw", [P, D_GROUP, TAIL])
        rows = sb("rows", [P, 2, D_GROUP, P], f32r)
        rows_t = sb("rows_t", [P, D_GROUP * P], f32r)
        x_own = sb("x_own", [P, D_GROUP * P])
        pairs = sb("pairs", [P, KQ, D_GROUP * P])
        select_raw = sb("select_raw", [P, 1 + KQ, P])
        select_r = sb("select_r", [P, 1 + KQ, P], f32r)
        w0m = sb("w0m", [P, KQ, MAPS])
        w0m_b = sb("w0m_b", [P, KQ, MAPS])
        w0t = sb("w0t", [P, MAPS])
        w0t_b = sb("w0t_b", [P, MAPS])
        w0t_hi = sb("w0t_hi", [P, MAPS], f32r)
        w0t_r = sb("w0t_r", [P, MAPS], f32r)
        ident = sb("ident", [P, P])
        ident_r = sb("ident_r", [P, P], f32r)
        c1_hi = sb("c1_hi", [P, 2, D_GROUP * P], f32r)
        c1_lo = sb("c1_lo", [P, 2, D_GROUP * P], f32r)
        w1_raw = sb("w1_raw", [P, FIELDS, MAPS])
        w1_hi = sb("w1_hi", [P, FIELDS * MAPS], f32r)
        w1_lo = sb("w1_lo", [P, FIELDS * MAPS], f32r)
        prod = sb("prod", [P, PROD_RING, BANK])
        gpair = sb("gpair", [P, 2 * BANK])
        gsum = sb("gsum", [P, D_GROUP, BANK])
        gfold = sb("gfold", [P, D_GROUP, BANK // 2])
        acc = sb("acc", [P, 2, D_GROUP, 2 * MAPS])
        c2 = sb("c2", [P, D_GROUP, MAPS])
        s1 = sb("s1", [P, TILES, D_GROUP * P])
        s2 = sb("s2", [P, TILES, D_GROUP * MAPS])
        wt1 = sb("wt1", [P, 2, HID1])
        wt1_d = sb("wt1_d", [DENSE, HID1])
        wt2 = sb("wt2", [P, HID1 // P, HID2])
        wt3 = sb("wt3", [P, HID2 // P])
        bt1 = sb("bt1", [P, HID1 // P])
        bt2 = sb("bt2", [P, HID2 // P])
        dense_sb = sb("dense", [P, TILES, DENSE])
        dense_t = sb("dense_t", [DENSE, BATCH])
        f1 = sb("f1", [P, BATCH])
        f2b = sb("f2b", [P, TILES, MAPS])
        f2 = sb("f2", [P, BATCH])
        s_half = sb("s_half", [P, 2, TILES, 2 * P])
        h1 = sb("h1", [P, HID1 // P, BATCH])
        h2 = sb("h2", [P, HID2 // P, BATCH])
        y_sb = sb("y", [1, BATCH])

        banks = [ctx.enter_context(nc.psum_tensor(f"bank{i}", [P, BANK], f32)) for i in range(8)]
        ps_turn, ps_c1 = banks[0], banks[1]
        ps_act, ps_dve = banks[2:2 + ACT_RING], banks[2 + ACT_RING:]

        ids_in, w0_in, w1_in, mlp_in = map(sem, ("ids_in", "w0_in", "w1_in", "mlp_in"))
        w0_zeroed, sums_zeroed, select_in = map(sem, ("w0_zeroed", "sums_zeroed", "select_in"))
        ids_staged, emb_first, emb_ready, settled = map(sem, ("ids_staged", "emb_first", "emb_ready", "settled"))
        gathered = [sem(f"gathered_{i}") for i in range(BLOCKS)]
        ident_steps, ident_ready, w0_steps, w1_hi_ready, w1_lo_ready = map(sem, ("ident_steps", "ident_ready", "w0_steps", "w1_hi_ready", "w1_lo_ready"))
        xs_ready, row_steps, pairs_ready, select_ready = map(sem, ("xs_ready", "row_steps", "pairs_ready", "select_ready"))
        turned, evacuated, l1_done = map(sem, ("turned", "evacuated", "l1_done"))
        hi_ready, lo_ready, c1_free = map(sem, ("hi_ready", "lo_ready", "c1_free"))
        act_full, dve_full, products, stt_done = map(sem, ("act_full", "dve_full", "products", "stt_done"))
        sums, folded, final_steps = map(sem, ("sums", "folded", "final_steps"))
        mlp_fold, mlp_turned, mlp_copied = map(sem, ("mlp_fold", "mlp_turned", "mlp_copied"))
        h1_full, h1_ready, h2_full, h2_ready = map(sem, ("h1_full", "h1_ready", "h2_full", "h2_ready"))
        y_full, y_ready, stored = map(sem, ("y_full", "y_ready", "stored"))
        ROW_STEPS = 5

        W0_DMAS, MLP_DMAS = 10, 7

        block = ctx.enter_context(nc.Block())

        @block.sync
        def _(sp):
            sp.dma_start(ids_sb[:, :, :], ids.rearrange("(t p) f -> p t f", p=P)).then_inc(ids_in, 16)
            sp.dma_start(w1_raw[:, :, :], w1.rearrange("(h m) n -> m h n", m=MAPS)).then_inc(w1_in, 16)
            sp.dma_start(wt1[:, :, :], w_top1[0:2 * P, :].rearrange("(k p) n -> p k n", p=P)).then_inc(mlp_in, 16)
            sp.dma_start(wt1_d[:, :], w_top1[2 * P:2 * P + DENSE, :]).then_inc(mlp_in, 16)
            sp.dma_start(wt2[:, :, :], w_top2.rearrange("(k p) n -> p k n", p=P)).then_inc(mlp_in, 16)
            sp.dma_start(wt3[:, :], w_top3.rearrange("(k p) o -> p (k o)", p=P),
                         allow_slow_non_contiguous=True).then_inc(mlp_in, 16)
            sp.dma_start(bt1[:, :], b_top1.rearrange("(k p) -> p k", p=P),
                         allow_slow_non_contiguous=True).then_inc(mlp_in, 16)
            sp.dma_start(bt2[:, :], b_top2.rearrange("(k p) -> p k", p=P),
                         allow_slow_non_contiguous=True).then_inc(mlp_in, 16)
            sp.dma_start(dense_sb[:, :, :], dense.rearrange("(t p) f -> p t f", p=P)).then_inc(mlp_in, 16)
            sp.wait_ge(y_ready, 2)
            sp.dma_start(out.rearrange("b o -> o b"), y_sb[:, :]).then_inc(stored, 16)
            sp.wait_ge(stored, 16)

        @block.gpsimd
        def _(pool):
            def wait(semaphore, value):
                if not isinstance(value, int) or value > 0:
                    pool.wait_ge(semaphore, value)

            def settle():
                pool.sem_inc(settled, 1)

            def gather(src_ids, f):
                nc.gpsimd.indirect_dma_start(
                    out=rows_next[:, f, :], out_offset=None, in_=tables[f],
                    in_offset=bass.IndirectOffsetOnAxis(ap=src_ids, axis=0)).then_inc(gathered[f // F_BLOCK], 16)

            def switch_tile(t):
                for block_sem in gathered:
                    pool.wait_ge(block_sem, 16 * F_BLOCK * (t + 1))
                pool.wait_ge(xs_ready, GROUPS_TILE * t)
                pool.wait_ge(row_steps, ROW_STEPS * GROUPS_TILE * t)
                settle()
                nc.gpsimd.tensor_copy(emb[:, :, :], rows_next[:, :, :].rearrange("p f d -> p d f")).then_inc(emb_ready, 1)
                pool.wait_ge(emb_ready, t)
                settle()

            def stage_rows(n, parity, d0):
                x = emb[:, d0:d0 + D_GROUP, :]
                x_hi = rows[:, parity, :, 0:FIELDS]
                spread = lambda ap: ap.unsqueeze(2).to_broadcast([P, D_GROUP, 2, TAIL])
                x_a, x_b = spread(x[:, :, 0:TAIL]), spread(x[:, :, TAIL:2 * TAIL])
                slots = rows[:, parity, :, TAIL_ROW:P].rearrange("p d (a s h) -> p d a s h", a=2, s=2)
                wait(row_steps, ROW_STEPS * n)
                settle()
                nc.gpsimd.tensor_copy(x_hi, x).then_inc(row_steps, 1)
                nc.gpsimd.tensor_tensor(out=tail_raw[:, :, :], in0=x[:, :, 0:TAIL], in1=x[:, :, TAIL:2 * TAIL],
                                        op=ALU.mult).then_inc(row_steps, 1)
                nc.gpsimd.tensor_tensor(out=slots[:, :, :, 0, :], in0=x_a, in1=x_b, op=ALU.mult).then_inc(row_steps, 1)
                pool.wait_ge(row_steps, ROW_STEPS * n + 1)
                nc.gpsimd.tensor_tensor(out=rows[:, parity, :, FIELDS:2 * FIELDS], in0=x, in1=x_hi.bitcast(f32),
                                        op=ALU.subtract).then_inc(row_steps, 1)
                pool.wait_ge(row_steps, ROW_STEPS * n + 3)
                nc.gpsimd.tensor_tensor(out=slots[:, :, :, 1, :], in0=spread(tail_raw[:, :, :]),
                                        in1=slots[:, :, :, 0, :].bitcast(f32), op=ALU.subtract).then_inc(row_steps, 1)

            def stage_scalars(d0, parity):
                nc.gpsimd.tensor_copy(xs[:, parity, :, :], emb[:, d0:d0 + D_GROUP, 0:FIELDS]).then_inc(xs_ready, 1)

            def add_products(g, c):
                wait(sums, SUM_N * g + 2 * c)
                if c == 0:
                    wait(folded, g)
                pool.wait_ge(products, ACT_N * g + ACT_C * (c + 1))
                both = prod[:, (c % 2) * ACT_C:(c % 2 + 1) * ACT_C, :].rearrange("p k n -> p (k n)")
                nc.gpsimd.tensor_tensor(out=gpair[:, :], in0=both[:, 0:2 * BANK], in1=both[:, 2 * BANK:4 * BANK],
                                        op=ALU.add).then_inc(sums, 1)
                pool.wait_ge(sums, SUM_N * g + 2 * c + 1)
                nc.gpsimd.tensor_tensor(out=gsum[:, c, :], in0=gpair[:, 0:BANK], in1=gpair[:, BANK:2 * BANK],
                                        op=ALU.add).then_inc(sums, 1)

            def fold(g):
                pool.wait_ge(sums, SUM_N * (g + 1))
                wait(final_steps, 3 * g)
                nc.gpsimd.tensor_tensor(out=gfold[:, :, :], in0=gsum[:, :, 0:BANK // 2], in1=gsum[:, :, BANK // 2:BANK],
                                        op=ALU.add).then_inc(folded, 1)

            nc.gpsimd.memset(ident[:, :], 0.0).then_inc(ident_steps, 1)
            pool.wait_ge(ident_steps, 1)
            nc.gpsimd.affine_select(out=ident[:, :], in_=ident[:, :], compare_op=ALU.not_equal, fill=1.0, base=0,
                                    pattern=[[-1, P]], channel_multiplier=1).then_inc(ident_steps, 1)
            pool.wait_ge(ids_in, 16)
            for f in range(FIELDS):
                gather(ids_sb[:, 0, f:f + 1], f)
            pool.wait_ge(emb_first, BLOCKS)
            stage_rows(0, 0, 0)
            stage_scalars(0, 0)
            stage_rows(1, 1, D_GROUP)

            def batch_tile(t, last):
                for j in range(GROUPS_TILE):
                    g = GROUPS_TILE * t + j
                    for c in range(D_GROUP):
                        q = D_GROUP * j + c
                        if not last:
                            if q == 0:
                                nc.gpsimd.tensor_copy(ids_next[:, :], ids_sb[:, t + 1, :]).then_inc(ids_staged, 1)
                                pool.wait_ge(ids_staged, t + 1)
                                settle()
                            if q < 24:
                                for f in range(q * FIELDS // 24, (q + 1) * FIELDS // 24):
                                    gather(ids_next[:, f:f + 1], f)
                        if c == 1 and not (last and j == GROUPS_TILE - 1):
                            wait(products, ACT_N * g)
                            wait(stt_done, STT_N * g)
                            settle()
                            stage_scalars(D_GROUP * ((j + 1) % GROUPS_TILE), (j + 1) % 2)
                        if c == 2 and not (last and j >= GROUPS_TILE - 2):
                            if j == GROUPS_TILE - 2:
                                switch_tile(t + 1)
                            pool.wait_ge(turned, USES * g + 1)
                            stage_rows(g + 2, j % 2, D_GROUP * ((j + 2) % GROUPS_TILE))
                        add_products(g, c)
                    fold(g)

            batch_tile(0, False)
            with pool.Fori(1, TILES - 1) as t:
                batch_tile(t, False)
            batch_tile(TILES - 1, True)

        @block.tensor
        def _(pe):
            def turn(n, parity, u):
                if u == 0:
                    pe.wait_ge(pairs_ready, KQ * n)
                    pe.wait_ge(row_steps, ROW_STEPS * (n + 1))
                    for d in range(D_GROUP):
                        last = nc.tensor.transpose(ps_turn[:, d * P:(d + 1) * P].bitcast(f32r), rows[:, parity, d, :], ident_r[:, :])
                else:
                    if u <= 2:
                        pe.wait_ge(evacuated, 2 * n + u)
                    else:
                        pe.wait_ge(pairs_ready, KQ * n + u - 2)
                    last = nc.tensor.matmul(ps_turn[:, :], select_r[:, u - 1, :], rows_t[:, :], start=True, stop=True)
                last.then_inc(turned, 1)

            def layer1(n, step):
                if step == 0:
                    pe.wait_ge(evacuated, 2 * n + 1)
                    pe.wait_ge(c1_free, n)
                    nc.tensor.matmul(ps_c1[:, :], w0t_r[:, :], rows_t[:, :], start=True, stop=False)
                else:
                    kq = step - 1
                    pe.wait_ge(pairs_ready, KQ * n + step)
                    last = nc.tensor.matmul(ps_c1[:, :], w0m[:, kq, :], pairs[:, kq, :], start=False, stop=step == KQ)
                    if step == KQ:
                        last.then_inc(l1_done, 1)

            def group(g, parity, first=False, last=False):
                pe.wait_ge(hi_ready, g + 1)
                pe.wait_ge(lo_ready, g + 1)
                for c in range(D_GROUP):
                    hi, lo = (x[:, parity, c * P:(c + 1) * P] for x in (c1_hi, c1_lo))
                    for hq in range(HQ):
                        if last and (c, hq) == (3, 0):
                            turn_features(EARLY)
                        if not last:
                            if (c, hq) in TURN_AT:
                                turn(g + 1, 1 - parity, TURN_AT[c, hq])
                            if (c, hq) in L1_AT:
                                layer1(g + 1, L1_AT[c, hq])
                        if hq in ACT_BANKS:
                            k = ACT_C * c + ACT_BANKS.index(hq)
                            if not (first and k < ACT_RING):
                                pe.wait_ge(products, ACT_N * g + k + 1 - ACT_RING)
                            bank, full = ps_act[k % ACT_RING], act_full
                        else:
                            k = DVE_C * c + DVE_BANKS.index(hq)
                            if not (first and k < DVE_RING):
                                pe.wait_ge(stt_done, STT_N * g + H_BANK * (k + 1 - DVE_RING))
                            bank, full = ps_dve[k % DVE_RING], dve_full
                        cols = slice(hq * BANK, (hq + 1) * BANK)
                        nc.tensor.matmul(bank[:, :], hi, w1_hi[:, cols], start=True, stop=False)
                        nc.tensor.matmul(bank[:, :], hi, w1_lo[:, cols], start=False, stop=False)
                        nc.tensor.matmul(bank[:, :], lo, w1_hi[:, cols], start=False, stop=True).then_inc(full, 1)

            def turn_features(tiles):
                part = mlp_part(tiles)
                if part == 0:
                    pe.wait_ge(mlp_in, 16 * MLP_DMAS)
                else:
                    pe.wait_ge(h2_ready, HID2 // P)
                for i, t in enumerate(range(tiles.start, tiles.stop)):
                    last = nc.tensor.transpose(ps_turn[0:DENSE, i * P:(i + 1) * P], dense_sb[:, t, :], ident[:, :])
                last.then_inc(mlp_turned, 1)
                pe.wait_ge(mlp_fold, 4 * (part + 1))
                for i, t in enumerate(range(tiles.start, tiles.stop)):
                    last = nc.tensor.transpose(ps_c1[:, i * P:(i + 1) * P], f2b[:, t, :], ident[:, :])
                last.then_inc(mlp_turned, 1)

            def mlp(tiles):
                part, cols = mlp_part(tiles), slice(tiles.start * P, tiles.stop * P)
                n = cols.stop - cols.start
                pe.wait_ge(mlp_copied, 2 * (part + 1))
                for m in range(HID1 // P):
                    if m == 2:
                        pe.wait_ge(products, ACT_N * GROUPS)
                    if m == 2 and part:
                        pe.wait_ge(y_ready, part)
                    maps, bank = slice(m * P, (m + 1) * P), banks[m]
                    nc.tensor.matmul(bank[:, 0:n], wt1[:, 0, maps], f1[:, cols], start=True, stop=False)
                    nc.tensor.matmul(bank[:, 0:n], wt1[:, 1, maps], f2[:, cols], start=False, stop=False)
                    nc.tensor.matmul(bank[:, 0:n], wt1_d[:, maps], dense_t[:, cols], start=False, stop=True).then_inc(h1_full, 1)
                for m in range(HID2 // P):
                    for k in range(HID1 // P):
                        if m == 0:
                            pe.wait_ge(h1_ready, HID1 // P * part + max(k, 1) + 1)
                        last = nc.tensor.matmul(banks[m][:, 0:n], wt2[:, k, m * P:(m + 1) * P], h1[:, k, cols],
                                                start=k == 0, stop=k == HID1 // P - 1)
                    last.then_inc(h2_full, 1)
                for k in range(HID2 // P):
                    pe.wait_ge(h2_ready, HID2 // P * part + k + 1)
                    last = nc.tensor.matmul(banks[2][0:1, 0:n], wt3[:, k:k + 1], h2[:, k, cols], start=k == 0, stop=k == HID2 // P - 1)
                last.then_inc(y_full, 1)

            pe.wait_ge(ident_steps, 2)
            pe.wait_ge(ident_ready, 1)
            pe.wait_ge(select_ready, 1)
            for u in range(USES):
                turn(0, 0, u)
            pe.wait_ge(w0_steps, 4)
            for step in range(KQ + 1):
                layer1(0, step)
            pe.wait_ge(w1_hi_ready, 1)
            pe.wait_ge(w1_lo_ready, 1)
            group(0, 0, first=True)
            with pe.Fori(0, (GROUPS - 2) // 2) as i:
                group(2 * i + 1, 1)
                group(2 * i + 2, 0)
            group(GROUPS - 1, 1, last=True)

            mlp(EARLY)
            turn_features(LATE)
            mlp(LATE)

        @block.scalar
        def _(act):
            act.dma_start(select_raw[:, :, :], select.rearrange("s p m -> p s m")).then_inc(select_in, 16)
            for src, dst in (w0_a, w0m), (w0_b, w0m_b):
                act.dma_start(dst[:, :, :], src[0:KQ * P, :].rearrange("(k p) n -> p k n", p=P)).then_inc(w0_in, 16)
            act.wait_ge(w0_zeroed, 2)
            for src, dst in (w0_a, w0t), (w0_b, w0t_b):
                for row in range(TAIL_ROW, P, TAIL):
                    act.dma_start(dst[row:row + TAIL, :], src[KQ * P:KQ * P + TAIL, :]).then_inc(w0_in, 16)
            act.wait_ge(w1_in, 16)
            nc.scalar.activation(w1_hi[:, :], w1_raw[:, :, :].rearrange("p h n -> p (h n)"), ACT.Copy).then_inc(w1_hi_ready, 1)

            def evacuate(n, u):
                if u == 0:
                    act.wait_ge(l1_done, n)
                else:
                    act.wait_ge(pairs_ready, KQ * n)
                act.wait_ge(turned, USES * n + u + 1)
                nc.scalar.activation((x_own if u else rows_t)[:, :], ps_turn[:, :], ACT.Copy).then_inc(evacuated, 1)

            def high_part(n, parity):
                act.wait_ge(l1_done, n + 1)
                nc.scalar.activation(c1_hi[:, parity, :], ps_c1[:, :], ACT.Relu).then_inc(hi_ready, 1)

            def group(g, parity, first=False, last=False):
                act.wait_ge(xs_ready, g + 1)
                for c in range(D_GROUP):
                    for hq in range(HQ):
                        if not last:
                            if TURN_AT.get((c, hq), 2) < 2:
                                evacuate(g + 1, TURN_AT[c, hq])
                            if (c, hq) == HIGH_AT:
                                high_part(g + 1, 1 - parity)
                        if hq not in ACT_BANKS:
                            continue
                        i = ACT_BANKS.index(hq)
                        k = ACT_C * c + i
                        if i == 0 and (c >= 2 or not first):
                            act.wait_ge(sums, SUM_N * g + 2 * (c - 2) + 1)
                        act.wait_ge(act_full, ACT_N * g + k + 1)
                        for j in range(H_BANK):
                            h = hq * H_BANK + j
                            cols = slice(j * MAPS, (j + 1) * MAPS)
                            last_product = nc.scalar.activation(prod[:, k % PROD_RING, cols], ps_act[k % ACT_RING][:, cols],
                                                                ACT.Copy, scale=xs[:, parity, c, h:h + 1])
                        last_product.then_inc(products, 1)

            def copy_features(tiles):
                part, cols = mlp_part(tiles), slice(tiles.start * P, tiles.stop * P)
                n = cols.stop - cols.start
                act.wait_ge(mlp_turned, 2 * part + 1)
                nc.scalar.activation(dense_t[:, cols], ps_turn[0:DENSE, 0:n], ACT.Copy).then_inc(mlp_copied, 1)
                act.wait_ge(mlp_turned, 2 * part + 2)
                nc.scalar.activation(f2[:, cols], ps_c1[:, 0:n], ACT.Copy).then_inc(mlp_copied, 1)

            for u in range(2):
                evacuate(0, u)
            high_part(0, 0)
            group(0, 0, first=True)
            with act.Fori(0, (GROUPS - 2) // 2) as i:
                group(2 * i + 1, 1)
                group(2 * i + 2, 0)
            group(GROUPS - 1, 1, last=True)
            copy_features(EARLY)
            for tiles in (EARLY, LATE):
                part, cols = mlp_part(tiles), slice(tiles.start * P, tiles.stop * P)
                n = cols.stop - cols.start
                if part:
                    copy_features(tiles)
                for m in range(HID1 // P):
                    act.wait_ge(h1_full, HID1 // P * part + m + 1)
                    nc.scalar.activation(h1[:, m, cols], banks[m][:, 0:n], ACT.Relu, bias=bt1[:, m:m + 1]).then_inc(h1_ready, 1)
                for m in range(HID2 // P):
                    act.wait_ge(h2_full, HID2 // P * part + m + 1)
                    nc.scalar.activation(h2[:, m, cols], banks[m][:, 0:n], ACT.Relu, bias=bt2[:, m:m + 1]).then_inc(h2_ready, 1)
                act.wait_ge(y_full, part + 1)
                nc.scalar.activation(y_sb[:, cols], banks[2][0:1, 0:n], ACT.Copy).then_inc(y_ready, 1)

        @block.vector
        def _(dve):
            nc.vector.memset(w0t[:, :], 0.0).then_inc(w0_zeroed, 1)
            nc.vector.memset(w0t_b[:, :], 0.0).then_inc(w0_zeroed, 1)
            nc.vector.memset(s1[:, :, :], 0.0).then_inc(sums_zeroed, 1)
            nc.vector.memset(s2[:, :, :], 0.0).then_inc(sums_zeroed, 1)
            dve.wait_ge(ident_steps, 2)
            nc.vector.tensor_copy(ident_r[:, :], ident[:, :]).then_inc(ident_ready, 1)
            dve.wait_ge(select_in, 16)
            nc.vector.tensor_copy(select_r[:, :, :], select_raw[:, :, :]).then_inc(select_ready, 1)
            dve.wait_ge(w0_in, 16 * W0_DMAS)
            nc.vector.memset(w0m_b[0:FIELDS, 0, :], 0.0).then_inc(w0_steps, 1)
            nc.vector.tensor_tensor(out=w0t[:, :], in0=w0t[:, :], in1=w0t_b[:, :], op=ALU.add).then_inc(w0_steps, 1)
            dve.wait_ge(w0_steps, 2)
            nc.vector.tensor_tensor(out=w0m[:, :, :], in0=w0m[:, :, :], in1=w0m_b[:, :, :], op=ALU.add)
            nc.vector.tensor_copy(w0t_hi[:, :], w0t[:, :])
            nc.vector.tensor_copy(w0t_r[:, :], w0t[:, :]).then_inc(w0_steps, 1)
            dve.wait_ge(w0_steps, 3)
            nc.vector.tensor_tensor(out=w0t_r[LOW_ROW:P, :], in0=w0t[LOW_ROW:P, :], in1=w0t_hi[LOW_ROW:P, :].bitcast(f32),
                                    op=ALU.subtract).then_inc(w0_steps, 1)
            dve.wait_ge(w1_hi_ready, 1)
            nc.vector.tensor_tensor(out=w1_lo[:, :], in0=w1_raw[:, :, :].rearrange("p h n -> p (h n)"),
                                    in1=w1_hi[:, :].bitcast(f32), op=ALU.subtract).then_inc(w1_lo_ready, 1)

            for i in range(BLOCKS):
                fields = slice(i * F_BLOCK, (i + 1) * F_BLOCK)
                dve.wait_ge(gathered[i], 16 * F_BLOCK)
                nc.vector.tensor_copy(emb[:, :, fields], rows_next[:, fields, :].rearrange("p f d -> p d f")).then_inc(emb_first, 1)

            def make_pairs(n, kq):
                if kq == 0:
                    dve.wait_ge(l1_done, n)
                    dve.wait_ge(evacuated, 2 * (n + 1))
                dve.wait_ge(turned, USES * n + kq + 3)
                nc.vector.tensor_tensor(out=pairs[:, kq, :], in0=ps_turn[:, :], in1=x_own[:, :],
                                        op=ALU.mult).then_inc(pairs_ready, 1)

            def low_part(n, parity, tile):
                dve.wait_ge(hi_ready, n + 1)
                nc.vector.scalar_tensor_tensor(out=c1_lo[:, parity, :], in0=ps_c1[:, :], scalar=0.0,
                                               in1=c1_hi[:, parity, :].bitcast(f32), op0=ALU.max,
                                               op1=ALU.subtract).then_inc(lo_ready, 1)
                dve.wait_ge(c1_free, n)
                nc.vector.scalar_tensor_tensor(out=s1[:, tile, :], in0=ps_c1[:, :], scalar=0.0, in1=s1[:, tile, :],
                                               op0=ALU.max, op1=ALU.add).then_inc(c1_free, 1)

            def finish(n, parity, tile, step):
                if step == 0:
                    dve.wait_ge(folded, n + 1)
                    nc.vector.tensor_tensor(out=acc[:, parity, :, :], in0=acc[:, parity, :, :], in1=gfold[:, :, :],
                                            op=ALU.add).then_inc(final_steps, 1)
                elif step == 1:
                    dve.wait_ge(final_steps, 3 * n + 1)
                    nc.vector.tensor_tensor(out=c2[:, :, :], in0=acc[:, parity, :, 0:MAPS],
                                            in1=acc[:, parity, :, MAPS:2 * MAPS], op=ALU.add).then_inc(final_steps, 1)
                else:
                    dve.wait_ge(final_steps, 3 * n + 2)
                    nc.vector.scalar_tensor_tensor(out=s2[:, tile, :], in0=c2[:, :, :].rearrange("p d n -> p (d n)"),
                                                   scalar=0.0, in1=s2[:, tile, :], op0=ALU.max,
                                                   op1=ALU.add).then_inc(final_steps, 1)

            def group(g, parity, tile_next, tile_before, first=False, last=False):
                dve.wait_ge(xs_ready, g + 1)
                for c in range(D_GROUP):
                    if c == D_GROUP - 1 and not first:
                        dve.wait_ge(final_steps, 3 * g)
                    i = 0
                    for hq in range(HQ):
                        if TURN_AT.get((c, hq), 0) >= 2 and not last:
                            make_pairs(g + 1, TURN_AT[c, hq] - 2)
                        if (c, hq) == LOW_AT and not last:
                            low_part(g + 1, 1 - parity, tile_next)
                        if last and (c, hq) == (2, 0):
                            fold_features(EARLY)
                        if hq in ACT_BANKS:
                            continue
                        k = DVE_C * c + DVE_BANKS.index(hq)
                        if c == 1 and not first and k > DVE_C:
                            finish(g - 1, 1 - parity, tile_before, k - DVE_C - 1)
                        dve.wait_ge(dve_full, DVE_N * g + k + 1)
                        bank = ps_dve[k % DVE_RING]
                        for j in range(H_BANK):
                            h = hq * H_BANK + j
                            half = acc[:, parity, c, (i % 2) * MAPS:(i % 2 + 1) * MAPS]
                            source = bank[:, j * MAPS:(j + 1) * MAPS]
                            x_h = xs[:, parity, c, h:h + 1]
                            if i < 2:
                                ins = nc.vector.tensor_scalar(half, source, x_h, None, ALU.mult)
                            else:
                                dve.wait_ge(stt_done, STT_N * g + H_BANK * k + j - 1)
                                ins = nc.vector.scalar_tensor_tensor(out=half, in0=source, scalar=x_h, in1=half,
                                                                     op0=ALU.mult, op1=ALU.add)
                            ins.then_inc(stt_done, 1)
                            i += 1

            def fold_features(tiles):
                part = mlp_part(tiles)
                f1_t = f1[:, :].rearrange("p (t b) -> p t b", t=TILES)
                for m, (src, dst) in enumerate(((s2, f2b[:, tiles, :]), (s1, f1_t[:, tiles, :]))):
                    nc.vector.tensor_tensor(out=s_half[:, m, tiles, :], in0=src[:, tiles, 0:2 * P],
                                            in1=src[:, tiles, 2 * P:4 * P], op=ALU.add).then_inc(mlp_fold, 1)
                    dve.wait_ge(mlp_fold, 4 * part + 2 * m + 1)
                    nc.vector.tensor_tensor(out=dst, in0=s_half[:, m, tiles, 0:P], in1=s_half[:, m, tiles, P:2 * P],
                                            op=ALU.add).then_inc(mlp_fold, 1)

            dve.wait_ge(sums_zeroed, 2)
            for kq in range(KQ):
                make_pairs(0, kq)
            low_part(0, 0, 0)
            group(0, 0, 0, 0, first=True)
            with dve.Fori(0, (GROUPS - 2) // 2) as i:
                group(2 * i + 1, 1, (i + 1) // 4, i // 4)
                group(2 * i + 2, 0, (2 * i + 3) // 8, (2 * i + 1) // 8)
            group(GROUPS - 1, 1, None, TILES - 1, last=True)
            dve.wait_ge(stt_done, STT_N * GROUPS)
            for step in range(3):
                finish(GROUPS - 1, 1, TILES - 1, step)
            dve.wait_ge(final_steps, 3 * GROUPS)

            fold_features(LATE)


def kernel(**inputs):
    import concourse.bacc as bacc
    from concourse.bass_utils import run_bass_kernel_spmd

    nc = bacc.Bacc("TRN2", target_bir_lowering=False, num_devices=1)
    h, k = np.arange(FIELDS)[None, :], np.arange(SHIFTS + 1)[:, None]
    other = (h + k) % FIELDS
    rows_a = (h * FIELDS + other).reshape(-1)[:SHIFTS * FIELDS + TAIL]
    rows_b = (other * FIELDS + h).reshape(-1)[:SHIFTS * FIELDS + TAIL]
    select = np.zeros((1 + KQ, P, KQ, FIELDS), np.float32)
    for s in range(1 + KQ):
        for a in range(P // FIELDS):
            for b in range(FIELDS):
                f = b if s == 0 else other[(s - 1) * (P // FIELDS) + a, b]
                select[s, [f, FIELDS + f], a, b] = 1.0
    filter_0 = np.asarray(inputs["L0_rec_filter_0"])[0]
    arrays = {"dense_ctx": inputs["dense_ctx"], "ids": inputs["ids"]}
    arrays |= {f"tbl_{f}": inputs[f"tbl_{f}"] for f in range(FIELDS)}
    arrays |= {name: inputs[name] for name in ("W_top1", "b_top1", "W_top2", "b_top2", "W_top3")}
    arrays |= {"w0_a": filter_0[rows_a], "w0_b": filter_0[rows_b],
               "select": select.reshape(1 + KQ, P, P), "w1": np.asarray(inputs["L0_rec_filter_1"])[0]}
    arrays = {name: np.ascontiguousarray(a) for name, a in arrays.items()}
    ap = {name: nc.dram_tensor(name, a.shape, mybir.dt.from_np(a.dtype), kind="ExternalInput").ap()
          for name, a in arrays.items()}
    y = nc.dram_tensor("y", (BATCH, 1), mybir.dt.float32, kind="ExternalOutput").ap()
    cin_tower(nc, ap["dense_ctx"], ap["ids"], [ap[f"tbl_{f}"] for f in range(FIELDS)], ap["W_top1"], ap["b_top1"],
              ap["W_top2"], ap["b_top2"], ap["W_top3"], ap["w0_a"], ap["w0_b"], ap["select"], ap["w1"], y)
    r = run_bass_kernel_spmd(nc, [arrays], core_ids=[0])
    return r.results[0]["y"]
```

```python
from contextlib import ExitStack

import numpy as np

import concourse.bass as bass
from concourse import mybir

BATCH, FIELDS, DIM, MAPS = 512, 32, 32, 128
DENSE, HID1, HID2 = 16, 512, 256
P = 128
TILES = BATCH // P
D_GROUP = 4
GROUPS_TILE = DIM // D_GROUP
GROUPS = TILES * GROUPS_TILE
CHUNKS = GROUPS * D_GROUP
SHIFTS = FIELDS // 2
TAIL = FIELDS // 2
KQ = SHIFTS * FIELDS // P
BANK = 512
H_BANK = BANK // MAPS
HQ = FIELDS // H_BANK
TAIL_ROWS = 4 * TAIL

ACT_BANKS = (0, 2, 4, 6)
DVE_BANKS = tuple(hq for hq in range(HQ) if hq not in ACT_BANKS)
ACT_C, DVE_C = len(ACT_BANKS), len(DVE_BANKS)
ACT_N, DVE_N = D_GROUP * ACT_C, D_GROUP * DVE_C
ACT_RING, DVE_RING, PROD_RING = 2, 4, 2 * ACT_C
STT_N = DVE_N * H_BANK
SUM_N = 2 * D_GROUP
assert ACT_C == 4 and ACT_N % ACT_RING == 0 and DVE_N % DVE_RING == 0 and ACT_N % PROD_RING == 0

TURN_AT = (3, 0)
WARM_UPS = 3
EVACUATE_AT = (3, 1)
PAIRS_AT = {(0, 3): 0, (0, 5): 1, (0, 7): 2, (1, 3): 3}
L1_AT = {(1, 0): 0, (1, 2): 1, (1, 5): 2, (2, 0): 3, (2, 3): 4}
HIGH_AT, LOW_AT = (2, 5), (2, 7)
BLOCKS = 4
F_BLOCK = FIELDS // BLOCKS
GATHER_CHUNKS = 22
EARLY = slice(0, TILES - 1)
LATE = slice(TILES - 1, TILES)


def mlp_part(tiles):
    return 0 if tiles == EARLY else 1


def cin_tower(nc, dense, ids, tables, w_top1, b_top1, w_top2, b_top2, w_top3, w0_a, w0_b, w1, out):
    f32, f32r, i32 = mybir.dt.float32, mybir.dt.float32r, mybir.dt.int32
    ALU, ACT = mybir.AluOpType, mybir.ActivationFunctionType

    with ExitStack() as ctx:
        def sb(name, shape, dt=f32):
            return ctx.enter_context(nc.sbuf_tensor("sb_" + name, shape, dt))

        def sem(name):
            return ctx.enter_context(nc.semaphore(name))

        ids_sb = sb("ids", [P, TILES, FIELDS], i32)
        ids_next = sb("ids_next", [P, FIELDS], i32)
        rows_next = sb("rows_next", [P, FIELDS, DIM])
        emb = sb("emb", [P, DIM, FIELDS])
        xs = sb("xs", [P, 2, D_GROUP, FIELDS])
        tail_raw = sb("tail_raw", [P, D_GROUP, TAIL])
        tails = sb("tails", [P, 2, D_GROUP * TAIL_ROWS], f32r)
        tails_t = sb("tails_t", [P, 2 * P], f32r)
        x_rows = sb("x_rows", [P, 2, P])
        x_t = sb("x_t", [P, P])
        x_own = sb("x_own", [P, D_GROUP * P])
        pairs = sb("pairs", [P, KQ, D_GROUP * P])
        w0m = sb("w0m", [P, KQ, MAPS])
        w0m_b = sb("w0m_b", [P, KQ, MAPS])
        w0t = sb("w0t", [P, MAPS])
        w0t_b = sb("w0t_b", [P, MAPS])
        w0t_hi = sb("w0t_hi", [P, MAPS], f32r)
        w0t_r = sb("w0t_r", [P, 2, MAPS], f32r)
        ident = sb("ident", [P, P])
        ident_r = sb("ident_r", [P, P], f32r)
        c1_hi = sb("c1_hi", [P, 2, D_GROUP * P], f32r)
        c1_lo = sb("c1_lo", [P, 2, D_GROUP * P], f32r)
        w1_raw = sb("w1_raw", [P, FIELDS, MAPS])
        w1_hi = sb("w1_hi", [P, FIELDS * MAPS], f32r)
        w1_lo = sb("w1_lo", [P, FIELDS * MAPS], f32r)
        prod = sb("prod", [P, PROD_RING, BANK])
        gpair = sb("gpair", [P, 2 * BANK])
        gsum = sb("gsum", [P, D_GROUP, BANK])
        gfold = sb("gfold", [P, D_GROUP, BANK // 2])
        acc = sb("acc", [P, 2, D_GROUP, 2 * MAPS])
        c2 = sb("c2", [P, D_GROUP, MAPS])
        s1 = sb("s1", [P, TILES, D_GROUP * P])
        s2 = sb("s2", [P, TILES, D_GROUP * MAPS])
        wt1 = sb("wt1", [P, 2, HID1])
        wt1_d = sb("wt1_d", [DENSE, HID1])
        wt2 = sb("wt2", [P, HID1 // P, HID2])
        wt3 = sb("wt3", [P, HID2 // P])
        bt1 = sb("bt1", [P, HID1 // P])
        bt2 = sb("bt2", [P, HID2 // P])
        dense_sb = sb("dense", [P, TILES, DENSE])
        dense_t = sb("dense_t", [DENSE, BATCH])
        f1 = sb("f1", [P, BATCH])
        f2b = sb("f2b", [P, TILES, MAPS])
        f2 = sb("f2", [P, BATCH])
        s_half = sb("s_half", [P, 2, TILES, 2 * P])
        h1 = sb("h1", [P, HID1 // P, BATCH])
        h2 = sb("h2", [P, HID2 // P, BATCH])
        y_sb = sb("y", [1, BATCH])

        banks = [ctx.enter_context(nc.psum_tensor(f"bank{i}", [P, BANK], f32)) for i in range(8)]
        ps_turn, ps_c1 = banks[0], banks[1]
        ps_act, ps_dve = banks[2:2 + ACT_RING], banks[2 + ACT_RING:]

        ids_in, w0_in, w1_in, mlp_in = map(sem, ("ids_in", "w0_in", "w1_in", "mlp_in"))
        sums_zeroed = sem("sums_zeroed")
        ids_staged, emb_first, emb_ready, settled = map(sem, ("ids_staged", "emb_first", "emb_ready", "settled"))
        gathered = [sem(f"gathered_{i}") for i in range(BLOCKS)]
        ident_steps, ident_ready, w0_steps, w1_hi_ready, w1_lo_ready = map(sem, ("ident_steps", "ident_ready", "w0_steps", "w1_hi_ready", "w1_lo_ready"))
        xs_ready, row_steps, pairs_ready, tail_used = map(sem, ("xs_ready", "row_steps", "pairs_ready", "tail_used"))
        turned, evacuated, l1_done = map(sem, ("turned", "evacuated", "l1_done"))
        written, own_spread, sp_settled = map(sem, ("written", "own_spread", "sp_settled"))
        spread = [sem(f"spread_{kq}") for kq in range(KQ)]
        hi_ready, lo_ready, c1_free = map(sem, ("hi_ready", "lo_ready", "c1_free"))
        act_full, dve_full, products, stt_done = map(sem, ("act_full", "dve_full", "products", "stt_done"))
        sums, folded, final_steps = map(sem, ("sums", "folded", "final_steps"))
        mlp_fold, mlp_turned, mlp_copied = map(sem, ("mlp_fold", "mlp_turned", "mlp_copied"))
        h1_full, h1_ready, h2_full, h2_ready = map(sem, ("h1_full", "h1_ready", "h2_full", "h2_ready"))
        y_full, y_ready, stored = map(sem, ("y_full", "y_ready", "stored"))
        ROW_STEPS = 4

        W0_DMAS, MLP_DMAS = 4, 7
        turned_x = nc.dram_tensor("turned_x", (2, 2 * FIELDS, D_GROUP * P), f32).ap()

        block = ctx.enter_context(nc.Block())

        @block.sync
        def _(sp):
            sp.dma_start(ids_sb[:, :, :], ids.rearrange("(t p) f -> p t f", p=P)).then_inc(ids_in, 16)
            sp.dma_start(w1_raw[:, :, :], w1.rearrange("(h m) n -> m h n", m=MAPS)).then_inc(w1_in, 16)
            sp.dma_start(wt1[:, :, :], w_top1[0:2 * P, :].rearrange("(k p) n -> p k n", p=P)).then_inc(mlp_in, 16)
            sp.dma_start(wt1_d[:, :], w_top1[2 * P:2 * P + DENSE, :]).then_inc(mlp_in, 16)
            sp.dma_start(wt2[:, :, :], w_top2.rearrange("(k p) n -> p k n", p=P)).then_inc(mlp_in, 16)
            sp.dma_start(wt3[:, :], w_top3.rearrange("(k p) o -> p (k o)", p=P),
                         allow_slow_non_contiguous=True).then_inc(mlp_in, 16)
            sp.dma_start(bt1[:, :], b_top1.rearrange("(k p) -> p k", p=P),
                         allow_slow_non_contiguous=True).then_inc(mlp_in, 16)
            sp.dma_start(bt2[:, :], b_top2.rearrange("(k p) -> p k", p=P),
                         allow_slow_non_contiguous=True).then_inc(mlp_in, 16)
            sp.dma_start(dense_sb[:, :, :], dense.rearrange("(t p) f -> p t f", p=P)).then_inc(mlp_in, 16)

            def spread_rows(n, parity):
                slot, row = turned_x[parity], D_GROUP * P
                if not isinstance(n, int) or n >= 2:
                    for loaded in (own_spread, *spread):
                        sp.wait_ge(loaded, 16 * (n - 1))
                        sp.sem_inc(sp_settled, 1)
                sp.wait_ge(evacuated, 2 * n + 1)
                sp.sem_inc(sp_settled, 1)
                for half in range(2):
                    dst = bass.AP(slot.tensor, slot.offset + half * FIELDS * row, [[P, D_GROUP], [row, FIELDS], [1, P]])
                    sp.dma_start(dst, x_t[:, :]).then_inc(written, 16)
                sp.wait_ge(written, 32 * (n + 1))
                sp.sem_inc(sp_settled, 1)
                if not isinstance(n, int) or n >= 1:
                    sp.wait_ge(pairs_ready, KQ * n)
                    sp.sem_inc(sp_settled, 1)
                own = bass.AP(slot.tensor, slot.offset, [[0, P // FIELDS], [row, FIELDS], [1, row]])
                sp.dma_start(x_own[:, :], own).then_inc(own_spread, 16)
                if not isinstance(n, int) or n >= 1:
                    sp.wait_ge(l1_done, n)
                    sp.sem_inc(sp_settled, 1)
                for kq in range(KQ):
                    src = bass.AP(slot.tensor, slot.offset + kq * P // FIELDS * row, [[row, P // FIELDS], [row, FIELDS], [1, row]])
                    sp.dma_start(pairs[:, kq, :], src).then_inc(spread[kq], 16)

            spread_rows(0, 0)
            spread_rows(1, 1)
            with sp.Fori(1, GROUPS // 2) as i:
                spread_rows(2 * i, 0)
                spread_rows(2 * i + 1, 1)
            sp.wait_ge(y_ready, 2)
            sp.dma_start(out.rearrange("b o -> o b"), y_sb[:, :]).then_inc(stored, 16)
            sp.wait_ge(stored, 16)

        @block.gpsimd
        def _(pool):
            def wait(semaphore, value):
                if not isinstance(value, int) or value > 0:
                    pool.wait_ge(semaphore, value)

            def settle():
                pool.sem_inc(settled, 1)

            def gather(src_ids, f):
                nc.gpsimd.indirect_dma_start(
                    out=rows_next[:, f, :], out_offset=None, in_=tables[f],
                    in_offset=bass.IndirectOffsetOnAxis(ap=src_ids, axis=0)).then_inc(gathered[f // F_BLOCK], 16)

            def switch_tile(t):
                for block_sem in gathered:
                    pool.wait_ge(block_sem, 16 * F_BLOCK * (t + 1))
                pool.wait_ge(xs_ready, GROUPS_TILE * t)
                pool.wait_ge(row_steps, ROW_STEPS * GROUPS_TILE * t)
                settle()
                nc.gpsimd.tensor_copy(emb[:, :, :], rows_next[:, :, :].rearrange("p f d -> p d f")).then_inc(emb_ready, 1)
                pool.wait_ge(emb_ready, t)
                settle()

            def stage_rows(n, parity, d0):
                x = emb[:, d0:d0 + D_GROUP, :]
                twice = lambda ap: ap.unsqueeze(2).to_broadcast([P, D_GROUP, 2, TAIL])
                x_a, x_b = twice(x[:, :, 0:TAIL]), twice(x[:, :, TAIL:2 * TAIL])
                slots = tails[:, parity, :].rearrange("p (d a s h) -> p d a s h", d=D_GROUP, a=2, s=2)
                wait(row_steps, ROW_STEPS * n)
                settle()
                nc.gpsimd.tensor_copy(x_rows[:, parity, :].rearrange("p (d f) -> p d f", d=D_GROUP), x).then_inc(row_steps, 1)
                nc.gpsimd.tensor_tensor(out=tail_raw[:, :, :], in0=x[:, :, 0:TAIL], in1=x[:, :, TAIL:2 * TAIL],
                                        op=ALU.mult).then_inc(row_steps, 1)
                nc.gpsimd.tensor_tensor(out=slots[:, :, :, 0, :], in0=x_a, in1=x_b, op=ALU.mult).then_inc(row_steps, 1)
                pool.wait_ge(row_steps, ROW_STEPS * n + 3)
                nc.gpsimd.tensor_tensor(out=slots[:, :, :, 1, :], in0=twice(tail_raw[:, :, :]),
                                        in1=slots[:, :, :, 0, :].bitcast(f32), op=ALU.subtract).then_inc(row_steps, 1)

            def stage_scalars(d0, parity):
                nc.gpsimd.tensor_copy(xs[:, parity, :, :], emb[:, d0:d0 + D_GROUP, 0:FIELDS]).then_inc(xs_ready, 1)

            def add_products(g, c):
                wait(sums, SUM_N * g + 2 * c)
                if c == 0:
                    wait(folded, g)
                pool.wait_ge(products, ACT_N * g + ACT_C * (c + 1))
                both = prod[:, (c % 2) * ACT_C:(c % 2 + 1) * ACT_C, :].rearrange("p k n -> p (k n)")
                nc.gpsimd.tensor_tensor(out=gpair[:, :], in0=both[:, 0:2 * BANK], in1=both[:, 2 * BANK:4 * BANK],
                                        op=ALU.add).then_inc(sums, 1)
                pool.wait_ge(sums, SUM_N * g + 2 * c + 1)
                nc.gpsimd.tensor_tensor(out=gsum[:, c, :], in0=gpair[:, 0:BANK], in1=gpair[:, BANK:2 * BANK],
                                        op=ALU.add).then_inc(sums, 1)

            def fold(g):
                pool.wait_ge(sums, SUM_N * (g + 1))
                wait(final_steps, 3 * g)
                nc.gpsimd.tensor_tensor(out=gfold[:, :, :], in0=gsum[:, :, 0:BANK // 2], in1=gsum[:, :, BANK // 2:BANK],
                                        op=ALU.add).then_inc(folded, 1)

            nc.gpsimd.memset(ident[:, :], 0.0).then_inc(ident_steps, 1)
            pool.wait_ge(ident_steps, 1)
            nc.gpsimd.affine_select(out=ident[:, :], in_=ident[:, :], compare_op=ALU.not_equal, fill=1.0, base=0,
                                    pattern=[[-1, P]], channel_multiplier=1).then_inc(ident_steps, 1)
            pool.wait_ge(ids_in, 16)
            for f in range(FIELDS):
                gather(ids_sb[:, 0, f:f + 1], f)
            pool.wait_ge(emb_first, BLOCKS)
            stage_rows(0, 0, 0)
            stage_scalars(0, 0)
            stage_rows(1, 1, D_GROUP)

            def batch_tile(t, last):
                for j in range(GROUPS_TILE):
                    g = GROUPS_TILE * t + j
                    for c in range(D_GROUP):
                        q = D_GROUP * j + c
                        if not last:
                            if q == 0:
                                nc.gpsimd.tensor_copy(ids_next[:, :], ids_sb[:, t + 1, :]).then_inc(ids_staged, 1)
                                pool.wait_ge(ids_staged, t + 1)
                                settle()
                            if q < GATHER_CHUNKS:
                                for f in range(q * FIELDS // GATHER_CHUNKS, (q + 1) * FIELDS // GATHER_CHUNKS):
                                    gather(ids_next[:, f:f + 1], f)
                        if c == 1 and not (last and j == GROUPS_TILE - 1):
                            wait(products, ACT_N * g)
                            wait(stt_done, STT_N * g)
                            settle()
                            stage_scalars(D_GROUP * ((j + 1) % GROUPS_TILE), (j + 1) % 2)
                        if c == 1 and not (last and j >= GROUPS_TILE - 2):
                            if j == GROUPS_TILE - 2:
                                switch_tile(t + 1)
                            pool.wait_ge(turned, 2 * g + 2)
                            stage_rows(g + 2, j % 2, D_GROUP * ((j + 2) % GROUPS_TILE))
                        add_products(g, c)
                    fold(g)

            batch_tile(0, False)
            with pool.Fori(1, TILES - 1) as t:
                batch_tile(t, False)
            batch_tile(TILES - 1, True)

        @block.tensor
        def _(pe):
            def turn(n, parity, bank=ps_turn):
                pe.wait_ge(row_steps, ROW_STEPS * n + 1)
                if not isinstance(n, int) or n >= 1:
                    pe.wait_ge(evacuated, 2 * n)
                nc.tensor.transpose(ps_turn[:, 0:P], x_rows[:, parity, :], ident[:, :]).then_inc(turned, 1)
                pe.wait_ge(row_steps, ROW_STEPS * (n + 1))
                for j in range(2):
                    last = nc.tensor.transpose(bank[:, (j + 1) * P:(j + 2) * P].bitcast(f32r),
                                               tails[:, parity, j * P:(j + 1) * P], ident_r[:, :])
                last.then_inc(turned, 1)

            def layer1(n, step):
                if step == 0:
                    pe.wait_ge(evacuated, 2 * n + 2)
                    if not isinstance(n, int) or n >= 1:
                        pe.wait_ge(c1_free, n)
                    by_parity = ps_c1[:, :].rearrange("p (j s b) -> p s j b", s=2, b=P)
                    for s in range(2):
                        last = nc.tensor.matmul(by_parity[:, s], w0t_r[:, s, :], tails_t[:, :], start=s == 0, stop=False)
                    last.then_inc(tail_used, 1)
                else:
                    kq = step - 1
                    pe.wait_ge(pairs_ready, KQ * n + step)
                    last = nc.tensor.matmul(ps_c1[:, :], w0m[:, kq, :], pairs[:, kq, :], start=False, stop=step == KQ)
                    if step == KQ:
                        last.then_inc(l1_done, 1)

            def group(g, parity, first=False, before_last=False, last=False):
                pe.wait_ge(hi_ready, g + 1)
                pe.wait_ge(lo_ready, g + 1)
                for c in range(D_GROUP):
                    hi, lo = (x[:, parity, c * P:(c + 1) * P] for x in (c1_hi, c1_lo))
                    for hq in range(HQ):
                        if last and (c, hq) == (3, 0):
                            turn_features(EARLY)
                        if (c, hq) == TURN_AT and not (last or before_last):
                            turn(g + 2, parity)
                        if not last:
                            if (c, hq) in L1_AT:
                                layer1(g + 1, L1_AT[c, hq])
                        if hq in ACT_BANKS:
                            k = ACT_C * c + ACT_BANKS.index(hq)
                            if not (first and k < ACT_RING):
                                pe.wait_ge(products, ACT_N * g + k + 1 - ACT_RING)
                            bank, full = ps_act[k % ACT_RING], act_full
                        else:
                            k = DVE_C * c + DVE_BANKS.index(hq)
                            if not (first and k < DVE_RING):
                                pe.wait_ge(stt_done, STT_N * g + H_BANK * (k + 1 - DVE_RING))
                            bank, full = ps_dve[k % DVE_RING], dve_full
                        cols = slice(hq * BANK, (hq + 1) * BANK)
                        nc.tensor.matmul(bank[:, :], hi, w1_hi[:, cols], start=True, stop=False)
                        nc.tensor.matmul(bank[:, :], hi, w1_lo[:, cols], start=False, stop=False)
                        nc.tensor.matmul(bank[:, :], lo, w1_hi[:, cols], start=False, stop=True).then_inc(full, 1)

            def turn_features(tiles):
                part = mlp_part(tiles)
                if part == 0:
                    pe.wait_ge(mlp_in, 16 * MLP_DMAS)
                else:
                    pe.wait_ge(h2_ready, HID2 // P)
                for i, t in enumerate(range(tiles.start, tiles.stop)):
                    last = nc.tensor.transpose(ps_turn[0:DENSE, i * P:(i + 1) * P], dense_sb[:, t, :], ident[:, :])
                last.then_inc(mlp_turned, 1)
                pe.wait_ge(mlp_fold, 4 * (part + 1))
                for i, t in enumerate(range(tiles.start, tiles.stop)):
                    last = nc.tensor.transpose(ps_c1[:, i * P:(i + 1) * P], f2b[:, t, :], ident[:, :])
                last.then_inc(mlp_turned, 1)

            def mlp(tiles):
                part, cols = mlp_part(tiles), slice(tiles.start * P, tiles.stop * P)
                n = cols.stop - cols.start
                pe.wait_ge(mlp_copied, 2 * (part + 1))
                for m in range(HID1 // P):
                    if m == 2:
                        pe.wait_ge(products, ACT_N * GROUPS)
                    if m == 2 and part:
                        pe.wait_ge(y_ready, part)
                    maps, bank = slice(m * P, (m + 1) * P), banks[m]
                    nc.tensor.matmul(bank[:, 0:n], wt1[:, 0, maps], f1[:, cols], start=True, stop=False)
                    nc.tensor.matmul(bank[:, 0:n], wt1[:, 1, maps], f2[:, cols], start=False, stop=False)
                    nc.tensor.matmul(bank[:, 0:n], wt1_d[:, maps], dense_t[:, cols], start=False, stop=True).then_inc(h1_full, 1)
                for m in range(HID2 // P):
                    for k in range(HID1 // P):
                        if m == 0:
                            pe.wait_ge(h1_ready, HID1 // P * part + max(k, 1) + 1)
                        last = nc.tensor.matmul(banks[m][:, 0:n], wt2[:, k, m * P:(m + 1) * P], h1[:, k, cols],
                                                start=k == 0, stop=k == HID1 // P - 1)
                    last.then_inc(h2_full, 1)
                for k in range(HID2 // P):
                    pe.wait_ge(h2_ready, HID2 // P * part + k + 1)
                    last = nc.tensor.matmul(banks[2][0:1, 0:n], wt3[:, k:k + 1], h2[:, k, cols], start=k == 0, stop=k == HID2 // P - 1)
                last.then_inc(y_full, 1)

            pe.wait_ge(ident_steps, 2)
            pe.wait_ge(ident_ready, 1)
            turn(0, 0, ps_act[0])
            turn(1, 1)
            pe.wait_ge(w0_steps, 7)
            for _ in range(WARM_UPS):
                nc.tensor.matmul(ps_dve[0][:, :], ident[:, :], w0m[:, :, :].rearrange("p k m -> p (k m)"), start=True, stop=True)
            for step in range(KQ + 1):
                layer1(0, step)
            pe.wait_ge(w1_hi_ready, 1)
            pe.wait_ge(w1_lo_ready, 1)
            group(0, 0, first=True)
            with pe.Fori(0, (GROUPS - 2) // 2 - 1) as i:
                group(2 * i + 1, 1)
                group(2 * i + 2, 0)
            group(GROUPS - 3, 1)
            group(GROUPS - 2, 0, before_last=True)
            group(GROUPS - 1, 1, last=True)

            mlp(EARLY)
            turn_features(LATE)
            mlp(LATE)

        @block.scalar
        def _(act):
            for src, dst in (w0_a, w0m), (w0_b, w0m_b):
                act.dma_start(dst[:, :, :], src[0:KQ * P, :].rearrange("(k p) n -> p k n", p=P)).then_inc(w0_in, 16)
            for src, dst in (w0_a, w0t), (w0_b, w0t_b):
                repeated = bass.AP(src.tensor, src.offset + KQ * P * MAPS, [[0, P // TAIL], [MAPS, TAIL], [1, MAPS]])
                act.dma_start(dst[:, :], repeated).then_inc(w0_in, 16)
            act.wait_ge(w1_in, 16)
            nc.scalar.activation(w1_hi[:, :], w1_raw[:, :, :].rearrange("p h n -> p (h n)"), ACT.Copy).then_inc(w1_hi_ready, 1)

            def evacuate(n, bank=ps_turn):
                later = not isinstance(n, int) or n >= 1
                act.wait_ge(turned, 2 * n + (2 if bank is ps_turn else 1))
                if later:
                    act.wait_ge(written, 32 * n)
                nc.scalar.activation(x_t[:, :], ps_turn[:, 0:P], ACT.Copy).then_inc(evacuated, 1)
                if bank is not ps_turn:
                    act.wait_ge(turned, 2 * n + 2)
                if later:
                    act.wait_ge(tail_used, n)
                nc.scalar.activation(tails_t[:, :], bank[:, P:3 * P], ACT.Copy).then_inc(evacuated, 1)

            def high_part(n, parity):
                act.wait_ge(l1_done, n + 1)
                nc.scalar.activation(c1_hi[:, parity, :], ps_c1[:, :], ACT.Relu).then_inc(hi_ready, 1)

            def group(g, parity, first=False, before_last=False, last=False):
                act.wait_ge(xs_ready, g + 1)
                for c in range(D_GROUP):
                    for hq in range(HQ):
                        if (c, hq) == EVACUATE_AT and not (last or before_last):
                            evacuate(g + 2)
                        if not last:
                            if (c, hq) == HIGH_AT:
                                high_part(g + 1, 1 - parity)
                        if hq not in ACT_BANKS:
                            continue
                        i = ACT_BANKS.index(hq)
                        k = ACT_C * c + i
                        if i == 0 and (c >= 2 or not first):
                            act.wait_ge(sums, SUM_N * g + 2 * (c - 2) + 1)
                        act.wait_ge(act_full, ACT_N * g + k + 1)
                        for j in range(H_BANK):
                            h = hq * H_BANK + j
                            cols = slice(j * MAPS, (j + 1) * MAPS)
                            last_product = nc.scalar.activation(prod[:, k % PROD_RING, cols], ps_act[k % ACT_RING][:, cols],
                                                                ACT.Copy, scale=xs[:, parity, c, h:h + 1])
                        last_product.then_inc(products, 1)

            def copy_features(tiles):
                part, cols = mlp_part(tiles), slice(tiles.start * P, tiles.stop * P)
                n = cols.stop - cols.start
                act.wait_ge(mlp_turned, 2 * part + 1)
                nc.scalar.activation(dense_t[:, cols], ps_turn[0:DENSE, 0:n], ACT.Copy).then_inc(mlp_copied, 1)
                act.wait_ge(mlp_turned, 2 * part + 2)
                nc.scalar.activation(f2[:, cols], ps_c1[:, 0:n], ACT.Copy).then_inc(mlp_copied, 1)

            evacuate(0, ps_act[0])
            high_part(0, 0)
            evacuate(1)
            group(0, 0, first=True)
            with act.Fori(0, (GROUPS - 2) // 2 - 1) as i:
                group(2 * i + 1, 1)
                group(2 * i + 2, 0)
            group(GROUPS - 3, 1)
            group(GROUPS - 2, 0, before_last=True)
            group(GROUPS - 1, 1, last=True)
            copy_features(EARLY)
            for tiles in (EARLY, LATE):
                part, cols = mlp_part(tiles), slice(tiles.start * P, tiles.stop * P)
                n = cols.stop - cols.start
                if part:
                    copy_features(tiles)
                for m in range(HID1 // P):
                    act.wait_ge(h1_full, HID1 // P * part + m + 1)
                    nc.scalar.activation(h1[:, m, cols], banks[m][:, 0:n], ACT.Relu, bias=bt1[:, m:m + 1]).then_inc(h1_ready, 1)
                for m in range(HID2 // P):
                    act.wait_ge(h2_full, HID2 // P * part + m + 1)
                    nc.scalar.activation(h2[:, m, cols], banks[m][:, 0:n], ACT.Relu, bias=bt2[:, m:m + 1]).then_inc(h2_ready, 1)
                act.wait_ge(y_full, part + 1)
                nc.scalar.activation(y_sb[:, cols], banks[2][0:1, 0:n], ACT.Copy).then_inc(y_ready, 1)

        @block.vector
        def _(dve):
            nc.vector.memset(s1[:, :, :], 0.0).then_inc(sums_zeroed, 1)
            nc.vector.memset(s2[:, :, :], 0.0).then_inc(sums_zeroed, 1)
            dve.wait_ge(ident_steps, 2)
            nc.vector.tensor_copy(ident_r[:, :], ident[:, :]).then_inc(ident_ready, 1)
            dve.wait_ge(w0_in, 16 * W0_DMAS)
            nc.vector.memset(w0m_b[0:FIELDS, 0, :], 0.0).then_inc(w0_steps, 1)
            nc.vector.tensor_tensor(out=w0t[:, :], in0=w0t[:, :], in1=w0t_b[:, :], op=ALU.add).then_inc(w0_steps, 1)
            dve.wait_ge(w0_steps, 2)
            nc.vector.tensor_tensor(out=w0m[:, :, :], in0=w0m[:, :, :], in1=w0m_b[:, :, :], op=ALU.add)
            nc.vector.tensor_copy(w0t_hi[:, :], w0t[:, :])
            dve.wait_ge(sums_zeroed, 1)
            nc.vector.tensor_copy(w0t_r[:, :, :].rearrange("p s m -> p (s m)"), s1[:, 0, 0:2 * MAPS]).then_inc(w0_steps, 1)
            dve.wait_ge(w0_steps, 3)
            for s in range(2):
                rows = slice(s * TAIL_ROWS, (s + 1) * TAIL_ROWS)
                nc.vector.tensor_copy(w0t_r[rows, s, :], w0t[rows, :]).then_inc(w0_steps, 1)
            dve.wait_ge(w0_steps, 5)
            for s in range(2):
                rows = slice(s * TAIL_ROWS + TAIL_ROWS // 2, (s + 1) * TAIL_ROWS)
                nc.vector.tensor_tensor(out=w0t_r[rows, s, :], in0=w0t[rows, :], in1=w0t_hi[rows, :].bitcast(f32),
                                        op=ALU.subtract).then_inc(w0_steps, 1)
            dve.wait_ge(w1_hi_ready, 1)
            nc.vector.tensor_tensor(out=w1_lo[:, :], in0=w1_raw[:, :, :].rearrange("p h n -> p (h n)"),
                                    in1=w1_hi[:, :].bitcast(f32), op=ALU.subtract).then_inc(w1_lo_ready, 1)

            for i in range(BLOCKS):
                fields = slice(i * F_BLOCK, (i + 1) * F_BLOCK)
                dve.wait_ge(gathered[i], 16 * F_BLOCK)
                nc.vector.tensor_copy(emb[:, :, fields], rows_next[:, fields, :].rearrange("p f d -> p d f")).then_inc(emb_first, 1)

            def make_pairs(n, kq):
                if kq == 0:
                    dve.wait_ge(own_spread, 16 * (n + 1))
                dve.wait_ge(spread[kq], 16 * (n + 1))
                nc.vector.tensor_tensor(out=pairs[:, kq, :], in0=pairs[:, kq, :], in1=x_own[:, :],
                                        op=ALU.mult).then_inc(pairs_ready, 1)

            def low_part(n, parity, tile):
                dve.wait_ge(hi_ready, n + 1)
                nc.vector.scalar_tensor_tensor(out=c1_lo[:, parity, :], in0=ps_c1[:, :], scalar=0.0,
                                               in1=c1_hi[:, parity, :].bitcast(f32), op0=ALU.max,
                                               op1=ALU.subtract).then_inc(lo_ready, 1)
                dve.wait_ge(c1_free, n)
                nc.vector.scalar_tensor_tensor(out=s1[:, tile, :], in0=ps_c1[:, :], scalar=0.0, in1=s1[:, tile, :],
                                               op0=ALU.max, op1=ALU.add).then_inc(c1_free, 1)

            def finish(n, parity, tile, step):
                if step == 0:
                    dve.wait_ge(folded, n + 1)
                    nc.vector.tensor_tensor(out=acc[:, parity, :, :], in0=acc[:, parity, :, :], in1=gfold[:, :, :],
                                            op=ALU.add).then_inc(final_steps, 1)
                elif step == 1:
                    dve.wait_ge(final_steps, 3 * n + 1)
                    nc.vector.tensor_tensor(out=c2[:, :, :], in0=acc[:, parity, :, 0:MAPS],
                                            in1=acc[:, parity, :, MAPS:2 * MAPS], op=ALU.add).then_inc(final_steps, 1)
                else:
                    dve.wait_ge(final_steps, 3 * n + 2)
                    nc.vector.scalar_tensor_tensor(out=s2[:, tile, :], in0=c2[:, :, :].rearrange("p d n -> p (d n)"),
                                                   scalar=0.0, in1=s2[:, tile, :], op0=ALU.max,
                                                   op1=ALU.add).then_inc(final_steps, 1)

            def group(g, parity, tile_next, tile_before, first=False, last=False):
                dve.wait_ge(xs_ready, g + 1)
                for c in range(D_GROUP):
                    if c == D_GROUP - 1 and not first:
                        dve.wait_ge(final_steps, 3 * g)
                    i = 0
                    for hq in range(HQ):
                        if (c, hq) in PAIRS_AT and not last:
                            make_pairs(g + 1, PAIRS_AT[c, hq])
                        if (c, hq) == LOW_AT and not last:
                            low_part(g + 1, 1 - parity, tile_next)
                        if last and (c, hq) == (2, 0):
                            fold_features(EARLY)
                        if hq in ACT_BANKS:
                            continue
                        k = DVE_C * c + DVE_BANKS.index(hq)
                        if c == 1 and not first and k > DVE_C:
                            finish(g - 1, 1 - parity, tile_before, k - DVE_C - 1)
                        dve.wait_ge(dve_full, DVE_N * g + k + 1)
                        bank = ps_dve[k % DVE_RING]
                        for j in range(H_BANK):
                            h = hq * H_BANK + j
                            half = acc[:, parity, c, (i % 2) * MAPS:(i % 2 + 1) * MAPS]
                            source = bank[:, j * MAPS:(j + 1) * MAPS]
                            x_h = xs[:, parity, c, h:h + 1]
                            if i < 2:
                                ins = nc.vector.tensor_scalar(half, source, x_h, None, ALU.mult)
                            else:
                                dve.wait_ge(stt_done, STT_N * g + H_BANK * k + j - 1)
                                ins = nc.vector.scalar_tensor_tensor(out=half, in0=source, scalar=x_h, in1=half,
                                                                     op0=ALU.mult, op1=ALU.add)
                            ins.then_inc(stt_done, 1)
                            i += 1

            def fold_features(tiles):
                part = mlp_part(tiles)
                f1_t = f1[:, :].rearrange("p (t b) -> p t b", t=TILES)
                for m, (src, dst) in enumerate(((s2, f2b[:, tiles, :]), (s1, f1_t[:, tiles, :]))):
                    nc.vector.tensor_tensor(out=s_half[:, m, tiles, :], in0=src[:, tiles, 0:2 * P],
                                            in1=src[:, tiles, 2 * P:4 * P], op=ALU.add).then_inc(mlp_fold, 1)
                    dve.wait_ge(mlp_fold, 4 * part + 2 * m + 1)
                    nc.vector.tensor_tensor(out=dst, in0=s_half[:, m, tiles, 0:P], in1=s_half[:, m, tiles, P:2 * P],
                                            op=ALU.add).then_inc(mlp_fold, 1)

            dve.wait_ge(sums_zeroed, 2)
            for kq in range(KQ):
                make_pairs(0, kq)
            low_part(0, 0, 0)
            group(0, 0, 0, 0, first=True)
            with dve.Fori(0, (GROUPS - 2) // 2) as i:
                group(2 * i + 1, 1, (i + 1) // 4, i // 4)
                group(2 * i + 2, 0, (2 * i + 3) // 8, (2 * i + 1) // 8)
            group(GROUPS - 1, 1, None, TILES - 1, last=True)
            dve.wait_ge(stt_done, STT_N * GROUPS)
            for step in range(3):
                finish(GROUPS - 1, 1, TILES - 1, step)
            dve.wait_ge(final_steps, 3 * GROUPS)

            fold_features(LATE)


def kernel(**inputs):
    import concourse.bacc as bacc
    from concourse.bass_utils import run_bass_kernel_spmd

    nc = bacc.Bacc("TRN2", target_bir_lowering=False, num_devices=1)
    h, k = np.arange(FIELDS)[None, :], np.arange(SHIFTS + 1)[:, None]
    other = (h + k) % FIELDS
    rows_a = (h * FIELDS + other).reshape(-1)[:SHIFTS * FIELDS + TAIL]
    rows_b = (other * FIELDS + h).reshape(-1)[:SHIFTS * FIELDS + TAIL]
    filter_0 = np.asarray(inputs["L0_rec_filter_0"])[0]
    arrays = {"dense_ctx": inputs["dense_ctx"], "ids": inputs["ids"]}
    arrays |= {f"tbl_{f}": inputs[f"tbl_{f}"] for f in range(FIELDS)}
    arrays |= {name: inputs[name] for name in ("W_top1", "b_top1", "W_top2", "b_top2", "W_top3")}
    arrays |= {"w0_a": filter_0[rows_a], "w0_b": filter_0[rows_b],
               "w1": np.asarray(inputs["L0_rec_filter_1"])[0]}
    arrays = {name: np.ascontiguousarray(a) for name, a in arrays.items()}
    ap = {name: nc.dram_tensor(name, a.shape, mybir.dt.from_np(a.dtype), kind="ExternalInput").ap()
          for name, a in arrays.items()}
    y = nc.dram_tensor("y", (BATCH, 1), mybir.dt.float32, kind="ExternalOutput").ap()
    cin_tower(nc, ap["dense_ctx"], ap["ids"], [ap[f"tbl_{f}"] for f in range(FIELDS)], ap["W_top1"], ap["b_top1"],
              ap["W_top2"], ap["b_top2"], ap["W_top3"], ap["w0_a"], ap["w0_b"], ap["w1"], y)
    r = run_bass_kernel_spmd(nc, [arrays], core_ids=[0])
    return r.results[0]["y"]
```

```python
from contextlib import ExitStack

import numpy as np

import concourse.bass as bass
from concourse import mybir

BATCH, FIELDS, DIM, MAPS = 512, 32, 32, 128
DENSE, HID1, HID2 = 16, 512, 256
P = 128
TILES = BATCH // P
D_GROUP = 4
GROUPS_TILE = DIM // D_GROUP
GROUPS = TILES * GROUPS_TILE
SHIFTS = FIELDS // 2
TAIL = FIELDS // 2
KQ = SHIFTS * FIELDS // P
BANK = 512
H_BANK = BANK // MAPS
HQ = FIELDS // H_BANK
TAIL_ROWS = 4 * TAIL

ACT_BANKS = (0, 2, 4, 6)
DVE_BANKS = tuple(hq for hq in range(HQ) if hq not in ACT_BANKS)
ACT_C, DVE_C = len(ACT_BANKS), len(DVE_BANKS)
ACT_N, DVE_N = D_GROUP * ACT_C, D_GROUP * DVE_C
ACT_RING, DVE_RING, PROD_RING = 2, 4, 2 * ACT_C
STT_N = DVE_N * H_BANK
SUM_N = 2 * D_GROUP
assert ACT_C == 4 and ACT_N % ACT_RING == 0 and DVE_N % DVE_RING == 0 and ACT_N % PROD_RING == 0

TURN_AT, EVACUATE_AT = (2, 3), (2, 4)
PAIRS_AT = {(0, 3): 0, (0, 5): 1, (0, 7): 2, (1, 1): 3}
PAIRS_HIGH_AT = {(1, 3): 2, (1, 5): 3}
PAIRS_LOW_AT = {(1, 7): 2, (2, 1): 3}
L1_AT = {(1, 1): 0, (1, 3): 1, (1, 6): 2, (2, 3): 3, (2, 6): 4}
HIGH_AT, LOW_AT = (3, 0), (3, 2)
SPLIT = tuple(PAIRS_HIGH_AT.values())
FIRST_DELAY = 3
WARM_UPS = 3
XS_RING = 4
STAGE_CHUNK, GATHER_CHUNKS, COPY_CHUNK = 0, (1, 2), 3
FIRST_GATHERS = 12
BLOCKS = 4
F_BLOCK = FIELDS // BLOCKS
EARLY = slice(0, TILES - 1)
LATE = slice(TILES - 1, TILES)


def place(chunk, bank, first):
    return divmod(HQ * chunk + bank - (FIRST_DELAY if first else 0), HQ)


def mlp_part(tiles):
    return 0 if tiles == EARLY else 1


def cin_tower(nc, dense, ids, tables, w_top1, b_top1, w_top2, b_top2, w_top3, w0_a, w0_b, w1, out):
    f32, f32r, i32 = mybir.dt.float32, mybir.dt.float32r, mybir.dt.int32
    ALU, ACT = mybir.AluOpType, mybir.ActivationFunctionType

    with ExitStack() as ctx:
        def sb(name, shape, dt=f32):
            return ctx.enter_context(nc.sbuf_tensor("sb_" + name, shape, dt))

        def sem(name):
            return ctx.enter_context(nc.semaphore(name))

        ids_sb = sb("ids", [P, TILES, FIELDS], i32)
        ids_next = sb("ids_next", [P, FIELDS], i32)
        emb = sb("emb", [P, 2, FIELDS, DIM])
        rows_next = sb("rows_next", [P, FIELDS, DIM])
        xs = sb("xs", [P, XS_RING, D_GROUP, FIELDS])
        tail_raw = sb("tail_raw", [P, D_GROUP, TAIL])
        tails = sb("tails", [P, 2, D_GROUP * TAIL_ROWS], f32r)
        tails_t = sb("tails_t", [P, 2 * P], f32r)
        x_t = sb("x_t", [P, P])
        x_own = sb("x_own", [P, D_GROUP * P])
        pairs = sb("pairs", [P, KQ, D_GROUP * P])
        w0m = sb("w0m", [P, KQ, MAPS])
        w0m_b = sb("w0m_b", [P, KQ, MAPS])
        pairs_hi = sb("pairs_hi", [P, len(SPLIT), D_GROUP * P], f32r)
        pairs_lo = sb("pairs_lo", [P, len(SPLIT), D_GROUP * P], f32r)
        w0m_hi = sb("w0m_hi", [P, KQ, MAPS], f32r)
        w0m_lo = sb("w0m_lo", [P, KQ, MAPS], f32r)
        w0t = sb("w0t", [P, MAPS])
        w0t_b = sb("w0t_b", [P, MAPS])
        w0t_hi = sb("w0t_hi", [P, MAPS], f32r)
        w0t_r = sb("w0t_r", [P, 2, MAPS], f32r)
        ident = sb("ident", [P, P])
        ident_r = sb("ident_r", [P, P], f32r)
        c1_hi = sb("c1_hi", [P, 2, D_GROUP * P], f32r)
        c1_lo = sb("c1_lo", [P, 2, D_GROUP * P], f32r)
        w1_raw = sb("w1_raw", [P, FIELDS, MAPS])
        w1_hi = sb("w1_hi", [P, FIELDS * MAPS], f32r)
        w1_lo = sb("w1_lo", [P, FIELDS * MAPS], f32r)
        prod = sb("prod", [P, PROD_RING, BANK])
        gpair = sb("gpair", [P, 2 * BANK])
        gsum = sb("gsum", [P, D_GROUP, BANK])
        gfold = sb("gfold", [P, D_GROUP, BANK // 2])
        acc = sb("acc", [P, 2, D_GROUP, 2 * MAPS])
        c2 = sb("c2", [P, D_GROUP, MAPS])
        s1 = sb("s1", [P, TILES, D_GROUP * P])
        s2 = sb("s2", [P, TILES, D_GROUP * MAPS])
        wt1 = sb("wt1", [P, 2, HID1])
        wt1_d = sb("wt1_d", [DENSE, HID1])
        wt2 = sb("wt2", [P, HID1 // P, HID2])
        wt3 = sb("wt3", [P, HID2 // P])
        bt1 = sb("bt1", [P, HID1 // P])
        bt2 = sb("bt2", [P, HID2 // P])
        dense_sb = sb("dense", [P, TILES, DENSE])
        dense_t = sb("dense_t", [DENSE, BATCH])
        f1 = sb("f1", [P, BATCH])
        f2b = sb("f2b", [P, TILES, MAPS])
        f2 = sb("f2", [P, BATCH])
        s_half = sb("s_half", [P, 2, TILES, 2 * P])
        w1_flat = w1_raw[:, :, :].rearrange("p h n -> p (h n)")
        h1 = w1_flat[:, 0:HID1 // P * BATCH].rearrange("p (k b) -> p k b", b=BATCH)
        h2 = w1_flat[:, HID1 // P * BATCH:(HID1 + HID2) // P * BATCH].rearrange("p (k b) -> p k b", b=BATCH)
        y_sb = sb("y", [1, BATCH])

        banks = [ctx.enter_context(nc.psum_tensor(f"bank{i}", [P, BANK], f32)) for i in range(8)]
        ps_turn, ps_c1 = banks[0], banks[1]
        ps_act, ps_dve = banks[2:2 + ACT_RING], banks[2 + ACT_RING:]

        ids_in, w0_in, w1_in, mlp_in = map(sem, ("ids_in", "w0_in", "w1_in", "mlp_in"))
        sums_zeroed = sem("sums_zeroed")
        ids_staged, copied, settled = map(sem, ("ids_staged", "copied", "settled"))
        gathered = [sem(f"gathered_{i}") for i in range(BLOCKS)]
        ident_steps, ident_ready, w0_steps, w1_hi_ready, w1_lo_ready = map(sem, ("ident_steps", "ident_ready", "w0_steps", "w1_hi_ready", "w1_lo_ready"))
        row_steps, pairs_ready, tail_used = map(sem, ("row_steps", "pairs_ready", "tail_used"))
        turned, evacuated, l1_done = map(sem, ("turned", "evacuated", "l1_done"))
        written, own_spread, sp_settled = map(sem, ("written", "own_spread", "sp_settled"))
        pairs_high, pairs_low = map(sem, ("pairs_high", "pairs_low"))
        spread = [sem(f"spread_{kq}") for kq in range(KQ)]
        hi_ready, lo_ready, c1_free = map(sem, ("hi_ready", "lo_ready", "c1_free"))
        act_full, dve_full, products, stt_done = map(sem, ("act_full", "dve_full", "products", "stt_done"))
        sums, folded, final_steps = map(sem, ("sums", "folded", "final_steps"))
        mlp_fold, mlp_turned, mlp_copied = map(sem, ("mlp_fold", "mlp_turned", "mlp_copied"))
        h1_full, h1_ready, h2_full, h2_ready = map(sem, ("h1_full", "h1_ready", "h2_full", "h2_ready"))
        y_full, y_ready, stored = map(sem, ("y_full", "y_ready", "stored"))
        ROW_STEPS = 4

        W0_DMAS, MLP_DMAS = 4, 7
        turned_x = nc.dram_tensor("turned_x", (2, 2 * FIELDS, D_GROUP * P), f32).ap()

        block = ctx.enter_context(nc.Block())

        @block.sync
        def _(sp):
            sp.dma_start(ids_sb[:, :, :], ids.rearrange("(t p) f -> p t f", p=P)).then_inc(ids_in, 16)
            sp.dma_start(w1_raw[:, :, :], w1.rearrange("(h m) n -> m h n", m=MAPS)).then_inc(w1_in, 16)
            sp.dma_start(wt1[:, :, :], w_top1[0:2 * P, :].rearrange("(k p) n -> p k n", p=P)).then_inc(mlp_in, 16)
            sp.dma_start(wt1_d[:, :], w_top1[2 * P:2 * P + DENSE, :]).then_inc(mlp_in, 16)
            sp.dma_start(wt2[:, :, :], w_top2.rearrange("(k p) n -> p k n", p=P)).then_inc(mlp_in, 16)
            sp.dma_start(wt3[:, :], w_top3.rearrange("(k p) o -> p (k o)", p=P),
                         allow_slow_non_contiguous=True).then_inc(mlp_in, 16)
            sp.dma_start(bt1[:, :], b_top1.rearrange("(k p) -> p k", p=P),
                         allow_slow_non_contiguous=True).then_inc(mlp_in, 16)
            sp.dma_start(bt2[:, :], b_top2.rearrange("(k p) -> p k", p=P),
                         allow_slow_non_contiguous=True).then_inc(mlp_in, 16)
            sp.dma_start(dense_sb[:, :, :], dense.rearrange("(t p) f -> p t f", p=P)).then_inc(mlp_in, 16)

            def spread_rows(n, parity):
                slot, row = turned_x[parity], D_GROUP * P
                if not isinstance(n, int) or n >= 2:
                    for loaded in (own_spread, *spread):
                        sp.wait_ge(loaded, 16 * (n - 1))
                        sp.sem_inc(sp_settled, 1)
                sp.wait_ge(evacuated, 2 * n + 1)
                sp.sem_inc(sp_settled, 1)
                for half in range(2):
                    dst = bass.AP(slot.tensor, slot.offset + half * FIELDS * row, [[P, D_GROUP], [row, FIELDS], [1, P]])
                    sp.dma_start(dst, x_t[:, :]).then_inc(written, 16)
                sp.wait_ge(written, 32 * (n + 1))
                sp.sem_inc(sp_settled, 1)
                if not isinstance(n, int) or n >= 1:
                    sp.wait_ge(pairs_ready, KQ * n)
                    sp.sem_inc(sp_settled, 1)
                own = bass.AP(slot.tensor, slot.offset, [[0, P // FIELDS], [row, FIELDS], [1, row]])
                sp.dma_start(x_own[:, :], own).then_inc(own_spread, 16)
                for kq in range(KQ) if isinstance(n, int) and n == 0 else (*SPLIT, *(kq for kq in range(KQ) if kq not in SPLIT)):
                    if not isinstance(n, int) or n >= 1:
                        if kq in SPLIT:
                            sp.wait_ge(pairs_low, len(SPLIT) * (n - 1) + SPLIT.index(kq) + 1)
                        else:
                            sp.wait_ge(l1_done, n)
                        sp.sem_inc(sp_settled, 1)
                    src = bass.AP(slot.tensor, slot.offset + kq * P // FIELDS * row, [[row, P // FIELDS], [row, FIELDS], [1, row]])
                    sp.dma_start(pairs[:, kq, :], src).then_inc(spread[kq], 16)

            spread_rows(0, 0)
            spread_rows(1, 1)
            with sp.Fori(1, GROUPS // 2) as i:
                spread_rows(2 * i, 0)
                spread_rows(2 * i + 1, 1)
            sp.wait_ge(y_ready, 2)
            sp.dma_start(out.rearrange("b o -> o b"), y_sb[:, :]).then_inc(stored, 16)
            sp.wait_ge(stored, 16)

        @block.gpsimd
        def _(pool):
            def wait(semaphore, value):
                if not isinstance(value, int) or value > 0:
                    pool.wait_ge(semaphore, value)

            def settle():
                pool.sem_inc(settled, 1)

            def gather(src_ids, dst, f):
                nc.gpsimd.indirect_dma_start(
                    out=dst[:, f, :], out_offset=None, in_=tables[f],
                    in_offset=bass.IndirectOffsetOnAxis(ap=src_ids, axis=0)).then_inc(gathered[f // F_BLOCK], 16)

            def copy_block(t, b):
                fields = slice(b * F_BLOCK, (b + 1) * F_BLOCK)
                pool.wait_ge(gathered[b], 16 * F_BLOCK * (t + 1))
                settle()
                nc.gpsimd.tensor_copy(emb[:, t % 2, fields, :], rows_next[:, fields, :]).then_inc(copied, 1)

            def await_tile(t):
                pool.wait_ge(copied, BLOCKS * t)
                settle()

            def stage_rows(n, tile, slot, parity, d0):
                x = xs[:, slot, :, :]
                twice = lambda ap: ap.unsqueeze(2).to_broadcast([P, D_GROUP, 2, TAIL])
                x_a, x_b = twice(x[:, :, 0:TAIL]), twice(x[:, :, TAIL:2 * TAIL])
                slots = tails[:, parity, :].rearrange("p (d a s h) -> p d a s h", d=D_GROUP, a=2, s=2)
                wait(row_steps, ROW_STEPS * n)
                settle()
                rows = emb[:, tile, :, d0:d0 + D_GROUP]
                nc.gpsimd.tensor_copy(x, rows.rearrange("p f d -> p d f")).then_inc(row_steps, 1)
                pool.wait_ge(row_steps, ROW_STEPS * n + 1)
                nc.gpsimd.tensor_tensor(out=tail_raw[:, :, :], in0=x[:, :, 0:TAIL], in1=x[:, :, TAIL:2 * TAIL],
                                        op=ALU.mult).then_inc(row_steps, 1)
                nc.gpsimd.tensor_tensor(out=slots[:, :, :, 0, :], in0=x_a, in1=x_b, op=ALU.mult).then_inc(row_steps, 1)
                pool.wait_ge(row_steps, ROW_STEPS * n + 3)
                nc.gpsimd.tensor_tensor(out=slots[:, :, :, 1, :], in0=twice(tail_raw[:, :, :]),
                                        in1=slots[:, :, :, 0, :].bitcast(f32), op=ALU.subtract).then_inc(row_steps, 1)

            def add_products(g, c):
                wait(sums, SUM_N * g + 2 * c)
                if c == 0:
                    wait(folded, g)
                pool.wait_ge(products, ACT_N * g + ACT_C * (c + 1))
                both = prod[:, (c % 2) * ACT_C:(c % 2 + 1) * ACT_C, :].rearrange("p k n -> p (k n)")
                nc.gpsimd.tensor_tensor(out=gpair[:, :], in0=both[:, 0:2 * BANK], in1=both[:, 2 * BANK:4 * BANK],
                                        op=ALU.add).then_inc(sums, 1)
                pool.wait_ge(sums, SUM_N * g + 2 * c + 1)
                nc.gpsimd.tensor_tensor(out=gsum[:, c, :], in0=gpair[:, 0:BANK], in1=gpair[:, BANK:2 * BANK],
                                        op=ALU.add).then_inc(sums, 1)

            def fold(g):
                pool.wait_ge(sums, SUM_N * (g + 1))
                wait(final_steps, 3 * g)
                nc.gpsimd.tensor_tensor(out=gfold[:, :, :], in0=gsum[:, :, 0:BANK // 2], in1=gsum[:, :, BANK // 2:BANK],
                                        op=ALU.add).then_inc(folded, 1)

            nc.gpsimd.memset(ident[:, :], 0.0).then_inc(ident_steps, 1)
            pool.wait_ge(ident_steps, 1)
            nc.gpsimd.affine_select(out=ident[:, :], in_=ident[:, :], compare_op=ALU.not_equal, fill=1.0, base=0,
                                    pattern=[[-1, P]], channel_multiplier=1).then_inc(ident_steps, 1)
            pool.wait_ge(ids_in, 16)
            for f in range(FIELDS):
                gather(ids_sb[:, 0, f:f + 1], emb[:, 0], f)
            for block_sem in gathered:
                pool.wait_ge(block_sem, 16 * F_BLOCK)
            stage_rows(0, 0, 0, 0, 0)
            stage_rows(1, 0, 1, 1, D_GROUP)

            def stage_ids(t):
                nc.gpsimd.tensor_copy(ids_next[:, :], ids_sb[:, t + 1, :]).then_inc(ids_staged, 1)
                pool.wait_ge(ids_staged, t + 1)
                settle()

            def fetch_next(c, t, i, groups, first=0):
                def gathered_by(part, parts):
                    return first + part * (FIELDS - first) // parts

                if c == COPY_CHUNK:
                    before = gathered_by(i - 1, groups) if i else 0
                    for b in range(BLOCKS):
                        if before < F_BLOCK * (b + 1) <= gathered_by(i, groups):
                            copy_block(t + 1, b)
                if c in GATHER_CHUNKS:
                    part, parts = len(GATHER_CHUNKS) * i + GATHER_CHUNKS.index(c), len(GATHER_CHUNKS) * groups
                    if part == 0 and first == 0:
                        stage_ids(t)
                    for f in range(gathered_by(part, parts), gathered_by(part + 1, parts)):
                        gather(ids_next[:, f:f + 1], rows_next, f)
                if (i, c) == (groups - 1, D_GROUP - 1):
                    copy_block(t + 1, BLOCKS - 1)

            def group(g, j, staged_tile, fetch=None, stage=True):
                for c in range(D_GROUP):
                    if c == STAGE_CHUNK and stage:
                        wait(products, ACT_N * (g - 1))
                        wait(stt_done, STT_N * (g - 1))
                        pool.wait_ge(turned, 2 * g + 2)
                        stage_rows(g + 2, staged_tile % 2, (j + 2) % XS_RING, j % 2, D_GROUP * ((j + 2) % GROUPS_TILE))
                    if fetch is not None:
                        fetch_next(c, *fetch)
                    add_products(g, c)
                fold(g)

            stage_ids(0)
            for f in range(FIRST_GATHERS):
                gather(ids_next[:, f:f + 1], rows_next, f)
            for g in range(GROUPS_TILE - 2):
                group(g, g, 0, fetch=(0, g, GROUPS_TILE - 2, FIRST_GATHERS))
            with pool.Fori(1, TILES - 1) as t:
                await_tile(t)
                for j in range(GROUPS_TILE):
                    group(GROUPS_TILE * t - 2 + j, (j - 2) % GROUPS_TILE, t, fetch=(t, j, GROUPS_TILE))
            await_tile(TILES - 1)
            for g in range(GROUPS - GROUPS_TILE - 2, GROUPS):
                group(g, g % GROUPS_TILE, TILES - 1, stage=g < GROUPS - 2)

        @block.tensor
        def _(pe):
            def turn(n, slot, parity, bank=ps_turn):
                pe.wait_ge(row_steps, ROW_STEPS * n + 1)
                if not isinstance(n, int) or n >= 1:
                    pe.wait_ge(evacuated, 2 * n)
                nc.tensor.transpose(ps_turn[:, 0:P], xs[:, slot, :, :].rearrange("p d f -> p (d f)"), ident[:, :]).then_inc(turned, 1)
                pe.wait_ge(row_steps, ROW_STEPS * (n + 1))
                for j in range(2):
                    last = nc.tensor.transpose(bank[:, (j + 1) * P:(j + 2) * P].bitcast(f32r),
                                               tails[:, parity, j * P:(j + 1) * P], ident_r[:, :])
                last.then_inc(turned, 1)

            def layer1(n, step):
                if step == 0:
                    pe.wait_ge(evacuated, 2 * n + 2)
                    if not isinstance(n, int) or n >= 1:
                        pe.wait_ge(c1_free, n)
                    by_parity = ps_c1[:, :].rearrange("p (j s b) -> p s j b", s=2, b=P)
                    for s in range(2):
                        last = nc.tensor.matmul(by_parity[:, s], w0t_r[:, s, :], tails_t[:, :], start=s == 0, stop=False)
                    last.then_inc(tail_used, 1)
                else:
                    kq = step - 1
                    if kq in SPLIT:
                        i = SPLIT.index(kq)
                        pe.wait_ge(pairs_high, len(SPLIT) * n + i + 1)
                        nc.tensor.matmul(ps_c1[:, :], w0m_hi[:, kq, :], pairs_hi[:, i, :], start=False, stop=False)
                        nc.tensor.matmul(ps_c1[:, :], w0m_lo[:, kq, :], pairs_hi[:, i, :], start=False, stop=False)
                        pe.wait_ge(pairs_low, len(SPLIT) * n + i + 1)
                        last = nc.tensor.matmul(ps_c1[:, :], w0m_hi[:, kq, :], pairs_lo[:, i, :], start=False, stop=step == KQ)
                    else:
                        pe.wait_ge(pairs_ready, KQ * n + kq + 1)
                        last = nc.tensor.matmul(ps_c1[:, :], w0m[:, kq, :], pairs[:, kq, :], start=False, stop=step == KQ)
                    if step == KQ:
                        last.then_inc(l1_done, 1)

            def group(g, slot, first=False, before_last=False, last=False):
                parity = slot % 2
                pe.wait_ge(hi_ready, g + 1)
                for c in range(D_GROUP):
                    hi, lo = (x[:, parity, c * P:(c + 1) * P] for x in (c1_hi, c1_lo))
                    for hq in range(HQ):
                        if last and (c, hq) == (3, 0):
                            turn_features(EARLY, ps_turn, ps_c1)
                        if (c, hq) == TURN_AT and not (last or before_last):
                            turn(g + 2, (slot + 2) % XS_RING, parity)
                        if not last:
                            if place(c, hq, first) in L1_AT:
                                layer1(g + 1, L1_AT[place(c, hq, first)])
                        if hq in ACT_BANKS:
                            k = ACT_C * c + ACT_BANKS.index(hq)
                            if not (first and k < ACT_RING):
                                pe.wait_ge(products, ACT_N * g + k + 1 - ACT_RING)
                            bank, full = ps_act[k % ACT_RING], act_full
                        else:
                            k = DVE_C * c + DVE_BANKS.index(hq)
                            if not (first and k < DVE_RING):
                                pe.wait_ge(stt_done, STT_N * g + H_BANK * (k + 1 - DVE_RING))
                            bank, full = ps_dve[k % DVE_RING], dve_full
                        cols = slice(hq * BANK, (hq + 1) * BANK)
                        nc.tensor.matmul(bank[:, :], hi, w1_hi[:, cols], start=True, stop=False)
                        nc.tensor.matmul(bank[:, :], hi, w1_lo[:, cols], start=False, stop=False)
                        if (c, hq) == (0, 0):
                            pe.wait_ge(lo_ready, g + 1)
                        nc.tensor.matmul(bank[:, :], lo, w1_hi[:, cols], start=False, stop=True).then_inc(full, 1)

            def turn_features(tiles, dense_bank, sum_bank):
                part = mlp_part(tiles)
                pe.wait_ge(mlp_in, 16 * MLP_DMAS)
                if part:
                    pe.wait_ge(stt_done, STT_N * GROUPS)
                for i, t in enumerate(range(tiles.start, tiles.stop)):
                    last = nc.tensor.transpose(dense_bank[0:DENSE, i * P:(i + 1) * P], dense_sb[:, t, :], ident[:, :])
                last.then_inc(mlp_turned, 1)
                pe.wait_ge(mlp_fold, 4 * (part + 1))
                for i, t in enumerate(range(tiles.start, tiles.stop)):
                    last = nc.tensor.transpose(sum_bank[:, i * P:(i + 1) * P], f2b[:, t, :], ident[:, :])
                last.then_inc(mlp_turned, 1)

            def mlp(tiles):
                part, cols = mlp_part(tiles), slice(tiles.start * P, tiles.stop * P)
                n = cols.stop - cols.start
                pe.wait_ge(mlp_copied, 2 * (part + 1))
                for m in range(HID1 // P):
                    if m == 2:
                        pe.wait_ge(products, ACT_N * GROUPS)
                    if m == 2 and part:
                        pe.wait_ge(y_ready, part)
                    maps, bank = slice(m * P, (m + 1) * P), banks[m]
                    nc.tensor.matmul(bank[:, 0:n], wt1[:, 0, maps], f1[:, cols], start=True, stop=False)
                    nc.tensor.matmul(bank[:, 0:n], wt1[:, 1, maps], f2[:, cols], start=False, stop=False)
                    nc.tensor.matmul(bank[:, 0:n], wt1_d[:, maps], dense_t[:, cols], start=False, stop=True).then_inc(h1_full, 1)
                for m in range(HID2 // P):
                    for k in range(HID1 // P):
                        if m == 0:
                            pe.wait_ge(h1_ready, HID1 // P * part + max(k, 1) + 1)
                        last = nc.tensor.matmul(banks[m][:, 0:n], wt2[:, k, m * P:(m + 1) * P], h1[:, k, cols],
                                                start=k == 0, stop=k == HID1 // P - 1)
                    last.then_inc(h2_full, 1)
                if tiles == EARLY:
                    turn_features(LATE, *ps_dve[:2])
                for k in range(HID2 // P):
                    pe.wait_ge(h2_ready, HID2 // P * part + k + 1)
                    last = nc.tensor.matmul(banks[2][0:1, 0:n], wt3[:, k:k + 1], h2[:, k, cols], start=k == 0, stop=k == HID2 // P - 1)
                last.then_inc(y_full, 1)

            pe.wait_ge(ident_steps, 2)
            pe.wait_ge(ident_ready, 1)
            turn(0, 0, 0, ps_act[0])
            turn(1, 1, 1)
            pe.wait_ge(w0_steps, 10)
            for _ in range(WARM_UPS):
                nc.tensor.matmul(ps_dve[0][:, :], ident[:, :], w0m[:, :, :].rearrange("p k m -> p (k m)"), start=True, stop=True)
            for step in range(KQ + 1):
                layer1(0, step)
            pe.wait_ge(w1_hi_ready, 1)
            pe.wait_ge(w1_lo_ready, 1)
            group(0, 0, first=True)
            with pe.Fori(0, (GROUPS - 4) // XS_RING) as i:
                for q in range(1, XS_RING + 1):
                    group(XS_RING * i + q, q % XS_RING)
            group(GROUPS - 3, 1)
            group(GROUPS - 2, 2, before_last=True)
            group(GROUPS - 1, 3, last=True)

            mlp(EARLY)
            mlp(LATE)

        @block.scalar
        def _(act):
            for src, dst in (w0_a, w0m), (w0_b, w0m_b):
                act.dma_start(dst[:, :, :], src[0:KQ * P, :].rearrange("(k p) n -> p k n", p=P)).then_inc(w0_in, 16)
            for src, dst in (w0_a, w0t), (w0_b, w0t_b):
                repeated = bass.AP(src.tensor, src.offset + KQ * P * MAPS, [[0, P // TAIL], [MAPS, TAIL], [1, MAPS]])
                act.dma_start(dst[:, :], repeated).then_inc(w0_in, 16)
            act.wait_ge(w1_in, 16)
            nc.scalar.activation(w1_hi[:, :], w1_raw[:, :, :].rearrange("p h n -> p (h n)"), ACT.Copy).then_inc(w1_hi_ready, 1)

            def evacuate(n, bank=ps_turn):
                later = not isinstance(n, int) or n >= 1
                act.wait_ge(turned, 2 * n + (2 if bank is ps_turn else 1))
                if later:
                    act.wait_ge(written, 32 * n)
                nc.scalar.activation(x_t[:, :], ps_turn[:, 0:P], ACT.Copy).then_inc(evacuated, 1)
                if bank is not ps_turn:
                    act.wait_ge(turned, 2 * n + 2)
                if later:
                    act.wait_ge(tail_used, n)
                nc.scalar.activation(tails_t[:, :], bank[:, P:3 * P], ACT.Copy).then_inc(evacuated, 1)

            def pairs_high_part(n, kq):
                if kq == SPLIT[0] and (not isinstance(n, int) or n >= 1):
                    act.wait_ge(l1_done, n)
                act.wait_ge(pairs_ready, KQ * n + kq + 1)
                nc.scalar.activation(pairs_hi[:, SPLIT.index(kq), :], pairs[:, kq, :], ACT.Copy).then_inc(pairs_high, 1)

            def high_part(n, parity):
                act.wait_ge(l1_done, n + 1)
                nc.scalar.activation(c1_hi[:, parity, :], ps_c1[:, :], ACT.Relu).then_inc(hi_ready, 1)

            def copy_features(tiles, dense_bank, sum_bank):
                part, cols = mlp_part(tiles), slice(tiles.start * P, tiles.stop * P)
                n = cols.stop - cols.start
                act.wait_ge(mlp_turned, 2 * part + 1)
                nc.scalar.activation(dense_t[:, cols], dense_bank[0:DENSE, 0:n], ACT.Copy).then_inc(mlp_copied, 1)
                act.wait_ge(mlp_turned, 2 * part + 2)
                nc.scalar.activation(f2[:, cols], sum_bank[:, 0:n], ACT.Copy).then_inc(mlp_copied, 1)

            def group(g, slot, first=False, before_last=False, last=False):
                parity = slot % 2
                act.wait_ge(row_steps, ROW_STEPS * g + 1)
                for c in range(D_GROUP):
                    for hq in range(HQ):
                        if last and (c, hq) == (3, 4):
                            copy_features(EARLY, ps_turn, ps_c1)
                        if (c, hq) == EVACUATE_AT and not (last or before_last):
                            evacuate(g + 2)
                        if not last:
                            if place(c, hq, first) in PAIRS_HIGH_AT:
                                pairs_high_part(g + 1, PAIRS_HIGH_AT[place(c, hq, first)])
                            if place(c, hq, first) == HIGH_AT:
                                high_part(g + 1, 1 - parity)
                        if hq not in ACT_BANKS:
                            continue
                        i = ACT_BANKS.index(hq)
                        k = ACT_C * c + i
                        if i == 0 and (c >= 2 or not first):
                            act.wait_ge(sums, SUM_N * g + 2 * (c - 2) + 1)
                        act.wait_ge(act_full, ACT_N * g + k + 1)
                        for j in range(H_BANK):
                            h = hq * H_BANK + j
                            cols = slice(j * MAPS, (j + 1) * MAPS)
                            last_product = nc.scalar.activation(prod[:, k % PROD_RING, cols], ps_act[k % ACT_RING][:, cols],
                                                                ACT.Copy, scale=xs[:, slot, c, h:h + 1])
                        last_product.then_inc(products, 1)

            evacuate(0, ps_act[0])
            for kq in SPLIT:
                pairs_high_part(0, kq)
            high_part(0, 0)
            evacuate(1)
            group(0, 0, first=True)
            with act.Fori(0, (GROUPS - 4) // XS_RING) as i:
                for q in range(1, XS_RING + 1):
                    group(XS_RING * i + q, q % XS_RING)
            group(GROUPS - 3, 1)
            group(GROUPS - 2, 2, before_last=True)
            group(GROUPS - 1, 3, last=True)
            for tiles in (EARLY, LATE):
                part, cols = mlp_part(tiles), slice(tiles.start * P, tiles.stop * P)
                n = cols.stop - cols.start
                for m in range(HID1 // P):
                    act.wait_ge(h1_full, HID1 // P * part + m + 1)
                    nc.scalar.activation(h1[:, m, cols], banks[m][:, 0:n], ACT.Relu, bias=bt1[:, m:m + 1]).then_inc(h1_ready, 1)
                for m in range(HID2 // P):
                    act.wait_ge(h2_full, HID2 // P * part + m + 1)
                    nc.scalar.activation(h2[:, m, cols], banks[m][:, 0:n], ACT.Relu, bias=bt2[:, m:m + 1]).then_inc(h2_ready, 1)
                if tiles == EARLY:
                    copy_features(LATE, *ps_dve[:2])
                act.wait_ge(y_full, part + 1)
                nc.scalar.activation(y_sb[:, cols], banks[2][0:1, 0:n], ACT.Copy).then_inc(y_ready, 1)

        @block.vector
        def _(dve):
            nc.vector.memset(s1[:, :, :], 0.0).then_inc(sums_zeroed, 1)
            nc.vector.memset(s2[:, :, :], 0.0).then_inc(sums_zeroed, 1)
            dve.wait_ge(ident_steps, 2)
            nc.vector.tensor_copy(ident_r[:, :], ident[:, :]).then_inc(ident_ready, 1)
            dve.wait_ge(w0_in, 16 * W0_DMAS)
            nc.vector.memset(w0m_b[0:FIELDS, 0, :], 0.0).then_inc(w0_steps, 1)
            nc.vector.tensor_tensor(out=w0t[:, :], in0=w0t[:, :], in1=w0t_b[:, :], op=ALU.add).then_inc(w0_steps, 1)
            dve.wait_ge(w0_steps, 2)
            nc.vector.tensor_tensor(out=w0m[:, :, :], in0=w0m[:, :, :], in1=w0m_b[:, :, :], op=ALU.add).then_inc(w0_steps, 1)
            nc.vector.tensor_copy(w0t_hi[:, :], w0t[:, :])
            dve.wait_ge(sums_zeroed, 1)
            nc.vector.tensor_copy(w0t_r[:, :, :].rearrange("p s m -> p (s m)"), s1[:, 0, 0:2 * MAPS]).then_inc(w0_steps, 1)
            dve.wait_ge(w0_steps, 4)
            for s in range(2):
                rows = slice(s * TAIL_ROWS, (s + 1) * TAIL_ROWS)
                nc.vector.tensor_copy(w0t_r[rows, s, :], w0t[rows, :]).then_inc(w0_steps, 1)
            nc.vector.tensor_copy(w0m_hi[:, :, :], w0m[:, :, :]).then_inc(w0_steps, 1)
            dve.wait_ge(w0_steps, 7)
            for s in range(2):
                rows = slice(s * TAIL_ROWS + TAIL_ROWS // 2, (s + 1) * TAIL_ROWS)
                nc.vector.tensor_tensor(out=w0t_r[rows, s, :], in0=w0t[rows, :], in1=w0t_hi[rows, :].bitcast(f32),
                                        op=ALU.subtract).then_inc(w0_steps, 1)
            nc.vector.tensor_tensor(out=w0m_lo[:, :, :], in0=w0m[:, :, :], in1=w0m_hi[:, :, :].bitcast(f32),
                                    op=ALU.subtract).then_inc(w0_steps, 1)
            dve.wait_ge(w1_hi_ready, 1)
            nc.vector.tensor_tensor(out=w1_lo[:, :], in0=w1_raw[:, :, :].rearrange("p h n -> p (h n)"),
                                    in1=w1_hi[:, :].bitcast(f32), op=ALU.subtract).then_inc(w1_lo_ready, 1)

            def make_pairs(n, kq):
                if kq == 0:
                    dve.wait_ge(own_spread, 16 * (n + 1))
                dve.wait_ge(spread[kq], 16 * (n + 1))
                nc.vector.tensor_tensor(out=pairs[:, kq, :], in0=pairs[:, kq, :], in1=x_own[:, :],
                                        op=ALU.mult).then_inc(pairs_ready, 1)

            def pairs_low_part(n, kq):
                i = SPLIT.index(kq)
                dve.wait_ge(pairs_high, len(SPLIT) * n + i + 1)
                nc.vector.tensor_tensor(out=pairs_lo[:, i, :], in0=pairs[:, kq, :], in1=pairs_hi[:, i, :].bitcast(f32),
                                        op=ALU.subtract).then_inc(pairs_low, 1)

            def low_part(n, parity, tile):
                dve.wait_ge(hi_ready, n + 1)
                nc.vector.scalar_tensor_tensor(out=c1_lo[:, parity, :], in0=ps_c1[:, :], scalar=0.0,
                                               in1=c1_hi[:, parity, :].bitcast(f32), op0=ALU.max,
                                               op1=ALU.subtract).then_inc(lo_ready, 1)
                dve.wait_ge(c1_free, n)
                nc.vector.scalar_tensor_tensor(out=s1[:, tile, :], in0=ps_c1[:, :], scalar=0.0, in1=s1[:, tile, :],
                                               op0=ALU.max, op1=ALU.add).then_inc(c1_free, 1)

            def finish(n, parity, tile, step):
                if step == 0:
                    dve.wait_ge(folded, n + 1)
                    nc.vector.tensor_tensor(out=acc[:, parity, :, :], in0=acc[:, parity, :, :], in1=gfold[:, :, :],
                                            op=ALU.add).then_inc(final_steps, 1)
                elif step == 1:
                    dve.wait_ge(final_steps, 3 * n + 1)
                    nc.vector.tensor_tensor(out=c2[:, :, :], in0=acc[:, parity, :, 0:MAPS],
                                            in1=acc[:, parity, :, MAPS:2 * MAPS], op=ALU.add).then_inc(final_steps, 1)
                else:
                    dve.wait_ge(final_steps, 3 * n + 2)
                    nc.vector.scalar_tensor_tensor(out=s2[:, tile, :], in0=c2[:, :, :].rearrange("p d n -> p (d n)"),
                                                   scalar=0.0, in1=s2[:, tile, :], op0=ALU.max,
                                                   op1=ALU.add).then_inc(final_steps, 1)

            def group(g, slot, tile_next, tile_before, first=False, last=False):
                parity = slot % 2
                dve.wait_ge(row_steps, ROW_STEPS * g + 1)
                for c in range(D_GROUP):
                    if c == D_GROUP - 1 and not first:
                        dve.wait_ge(final_steps, 3 * g)
                    i = 0
                    for hq in range(HQ):
                        if place(c, hq, first) in PAIRS_AT and not last:
                            make_pairs(g + 1, PAIRS_AT[place(c, hq, first)])
                        if place(c, hq, first) in PAIRS_LOW_AT and not last:
                            pairs_low_part(g + 1, PAIRS_LOW_AT[place(c, hq, first)])
                        if place(c, hq, first) == LOW_AT and not last:
                            low_part(g + 1, 1 - parity, tile_next)
                        if last and (c, hq) == (2, 0):
                            fold_features(EARLY)
                        if hq in ACT_BANKS:
                            continue
                        k = DVE_C * c + DVE_BANKS.index(hq)
                        if c == 1 and not first and k > DVE_C:
                            finish(g - 1, 1 - parity, tile_before, k - DVE_C - 1)
                        dve.wait_ge(dve_full, DVE_N * g + k + 1)
                        bank = ps_dve[k % DVE_RING]
                        for j in range(H_BANK):
                            h = hq * H_BANK + j
                            half = acc[:, parity, c, (i % 2) * MAPS:(i % 2 + 1) * MAPS]
                            source = bank[:, j * MAPS:(j + 1) * MAPS]
                            x_h = xs[:, slot, c, h:h + 1]
                            if i < 2:
                                ins = nc.vector.tensor_scalar(half, source, x_h, None, ALU.mult)
                            else:
                                dve.wait_ge(stt_done, STT_N * g + H_BANK * k + j - 1)
                                ins = nc.vector.scalar_tensor_tensor(out=half, in0=source, scalar=x_h, in1=half,
                                                                     op0=ALU.mult, op1=ALU.add)
                            ins.then_inc(stt_done, 1)
                            i += 1

            def fold_features(tiles):
                part = mlp_part(tiles)
                f1_t = f1[:, :].rearrange("p (t b) -> p t b", t=TILES)
                for m, (src, dst) in enumerate(((s2, f2b[:, tiles, :]), (s1, f1_t[:, tiles, :]))):
                    nc.vector.tensor_tensor(out=s_half[:, m, tiles, :], in0=src[:, tiles, 0:2 * P],
                                            in1=src[:, tiles, 2 * P:4 * P], op=ALU.add).then_inc(mlp_fold, 1)
                    dve.wait_ge(mlp_fold, 4 * part + 2 * m + 1)
                    nc.vector.tensor_tensor(out=dst, in0=s_half[:, m, tiles, 0:P], in1=s_half[:, m, tiles, P:2 * P],
                                            op=ALU.add).then_inc(mlp_fold, 1)

            dve.wait_ge(sums_zeroed, 2)
            for kq in range(KQ):
                make_pairs(0, kq)
            for kq in PAIRS_LOW_AT.values():
                pairs_low_part(0, kq)
            low_part(0, 0, 0)
            group(0, 0, 0, 0, first=True)
            with dve.Fori(0, (GROUPS - 4) // XS_RING) as i:
                for q in range(1, XS_RING + 1):
                    g = XS_RING * i + q
                    group(g, q % XS_RING, (g + 1) // GROUPS_TILE, (g - 1) // GROUPS_TILE)
            for g in range(GROUPS - 3, GROUPS):
                group(g, g % XS_RING, (g + 1) // GROUPS_TILE, (g - 1) // GROUPS_TILE, last=g == GROUPS - 1)
            dve.wait_ge(stt_done, STT_N * GROUPS)
            for step in range(3):
                finish(GROUPS - 1, 1, TILES - 1, step)
            dve.wait_ge(final_steps, 3 * GROUPS)

            fold_features(LATE)


def kernel(**inputs):
    import concourse.bacc as bacc
    from concourse.bass_utils import run_bass_kernel_spmd

    nc = bacc.Bacc("TRN2", target_bir_lowering=False, num_devices=1)
    h, k = np.arange(FIELDS)[None, :], np.arange(SHIFTS + 1)[:, None]
    other = (h + k) % FIELDS
    rows_a = (h * FIELDS + other).reshape(-1)[:SHIFTS * FIELDS + TAIL]
    rows_b = (other * FIELDS + h).reshape(-1)[:SHIFTS * FIELDS + TAIL]
    filter_0 = np.asarray(inputs["L0_rec_filter_0"])[0]
    arrays = {"dense_ctx": inputs["dense_ctx"], "ids": inputs["ids"]}
    arrays |= {f"tbl_{f}": inputs[f"tbl_{f}"] for f in range(FIELDS)}
    arrays |= {name: inputs[name] for name in ("W_top1", "b_top1", "W_top2", "b_top2", "W_top3")}
    arrays |= {"w0_a": filter_0[rows_a], "w0_b": filter_0[rows_b],
               "w1": np.asarray(inputs["L0_rec_filter_1"])[0]}
    arrays = {name: np.ascontiguousarray(a) for name, a in arrays.items()}
    ap = {name: nc.dram_tensor(name, a.shape, mybir.dt.from_np(a.dtype), kind="ExternalInput").ap()
          for name, a in arrays.items()}
    y = nc.dram_tensor("y", (BATCH, 1), mybir.dt.float32, kind="ExternalOutput").ap()
    cin_tower(nc, ap["dense_ctx"], ap["ids"], [ap[f"tbl_{f}"] for f in range(FIELDS)], ap["W_top1"], ap["b_top1"],
              ap["W_top2"], ap["b_top2"], ap["W_top3"], ap["w0_a"], ap["w0_b"], ap["w1"], y)
    r = run_bass_kernel_spmd(nc, [arrays], core_ids=[0])
    return r.results[0]["y"]
```
